# Optimizing a Trainium2 kernel written in Bass

```python
import numpy as np
import jax
import jax.numpy as jnp

def _softmax(x, axis=-1):
    return jax.nn.softmax(x, axis=axis)

def _gelu(x):
    return jax.nn.gelu(x, approximate=True)

def _silu(x):
    return jax.nn.silu(x)

def _sigmoid(x):
    return jax.nn.sigmoid(x)

def _layernorm(x, axis=-1, eps=1e-05):
    m = jnp.mean(x, axis=axis, keepdims=True)
    v = jnp.var(x, axis=axis, keepdims=True)
    return (x - m) / jnp.sqrt(v + eps)

def _scatter_add(tgt, idx, src, axis=0):
    return tgt.at[idx].add(src)

def _segment_sum(src, seg, n):
    return jax.ops.segment_sum(src, seg, n)
kernel_name = 'mk_seq_postln_d1_jaxref_r2_810fc7'

def setup_inputs(seed: int=0):
    np.random.seed(seed)
    _w = jnp.asarray

    def _L0_attn_setup():
        import jax, jax.numpy as jnp
        import numpy as np
        NUM_HEADS = 16
        key = jax.random.key(seed)
        kx, kq, kk, kv = jax.random.split(key, 4)
        N, S, D = (2, 2048, 512)
        scale = 1.0 / np.sqrt(D)
        x = jax.random.normal(kx, (N, S, D), dtype=jnp.float32)
        Wq = jax.random.normal(kq, (D, D), dtype=jnp.float32) * scale
        Wk = jax.random.normal(kk, (D, D), dtype=jnp.float32) * scale
        Wv = jax.random.normal(kv, (D, D), dtype=jnp.float32) * scale
        return {'x': x, 'Wq': Wq, 'Wk': Wk, 'Wv': Wv}
    _L0_attn_in = _L0_attn_setup()

    def _L0_ffn_setup():
        import jax, jax.numpy as jnp
        import numpy as np
        MAX_VAL = 100.0
        key = jax.random.key(seed)
        k1, k2, k3 = jax.random.split(key, 3)
        B, S, D_IN, D_OUT = (4, 4096, 512, 512)
        x = jax.random.normal(k1, (B, S, D_IN), dtype=jnp.float32)
        weights = jax.random.normal(k2, (D_OUT, D_IN), dtype=jnp.float32)
        scale = jnp.ones((D_OUT,), dtype=jnp.float32)
        bias = jax.random.normal(k3, (D_OUT,), dtype=jnp.float32)
        return {'x': x, 'weights': weights, 'scale': scale, 'bias': bias}
    _L0_ffn_in = _L0_ffn_setup()
    _d = {'L0_attn_x': _L0_attn_in['x'], 'L0_attn_Wq': _L0_attn_in['Wq'], 'L0_attn_Wk': _L0_attn_in['Wk'], 'L0_attn_Wv': _L0_attn_in['Wv'], 'L0_ffn_weights': _L0_ffn_in['weights'], 'L0_ffn_scale': _L0_ffn_in['scale'], 'L0_ffn_bias': _L0_ffn_in['bias']}
    _x0 = _d['L0_attn_x']
    _d['L0_attn_x'] = jax.random.normal(jax.random.fold_in(jax.random.key(seed), 1), (4, 2048, 512), dtype=_x0.dtype)
    del _x0
    return _d

def reference(L0_attn_x, L0_attn_Wq, L0_attn_Wk, L0_attn_Wv, L0_ffn_weights, L0_ffn_scale, L0_ffn_bias):

    def _L0_attn_ref(x, Wq, Wk, Wv):
        import jax, jax.numpy as jnp
        import numpy as np
        NUM_HEADS = 16
        N, S, D = x.shape
        H = NUM_HEADS
        hd = D // H
        q = (x @ Wq.T).reshape(N, S, H, hd).transpose(0, 2, 1, 3)
        k = (x @ Wk.T).reshape(N, S, H, hd).transpose(0, 2, 1, 3)
        v = (x @ Wv.T).reshape(N, S, H, hd).transpose(0, 2, 1, 3)
        energy = jnp.einsum('nhqd,nhkd->nhqk', q, k)
        attn = jax.nn.softmax(energy / jnp.sqrt(jnp.float32(hd)), axis=3)
        out = jnp.einsum('nhql,nhld->nhqd', attn, v)
        return out.transpose(0, 2, 1, 3).reshape(N, S, D)

    def _L0_ffn_ref(x, weights, scale, bias):
        import jax, jax.numpy as jnp
        import numpy as np
        MAX_VAL = 100.0
        w = (weights >= 0.0).astype(x.dtype) * 2.0 - 1.0
        y = jnp.einsum('bsi,oi->bso', x, w)
        y = y * scale + bias
        y = jnp.clip(y, -MAX_VAL, MAX_VAL)
        return y
    x = L0_attn_x
    x = _layernorm(x + _L0_attn_ref(x, L0_attn_Wq, L0_attn_Wk, L0_attn_Wv), axis=-1)
    x = _layernorm(x + _L0_ffn_ref(x, L0_ffn_weights, L0_ffn_scale, L0_ffn_bias), axis=-1)
    return x

_drawn_inputs = setup_inputs


def setup_inputs(seed=0):
    import zlib

    import numpy as np

    out = dict(_drawn_inputs(seed))
    spreads = {'L0_ffn_scale': (1.0, 0.2)}
    factors = {}
    for name, (base, spread) in spreads.items():
        noise = np.random.default_rng([zlib.crc32(name.encode()), seed]).standard_normal(out[name].shape)
        drawn = base * np.exp(spread * noise) if base else spread * noise
        out[name] = jnp.asarray(drawn.astype(out[name].dtype))
    for name, factor in factors.items():
        out[name] = (out[name] * factor).astype(out[name].dtype)
    return out
```

```python
import concourse.bass as bass
from concourse import mybir
from contextlib import ExitStack

FP32 = mybir.dt.float32
FP32R = mybir.dt.float32r
BF16 = mybir.dt.bfloat16
INT32 = mybir.dt.int32
ALU = mybir.AluOpType
ACT = mybir.ActivationFunctionType
AX = mybir.AxisListType

P = 128
N, S, D = 4, 2048, 512
H, HD = 16, 32
G = P // HD
NG = H // G
DC = D // P
BLK = 512
TPB = BLK // P
NBLK = N * S // BLK
QB = S // BLK
KT = S // P
ITEMS = N * NG
SCALE = float(HD) ** -0.5
EPS = 1e-5
MAX_VAL = 100.0
KROWS = 3 * HD + 2
SHIFT = 0.25
BOUND_MAX = 64.0
BOUND_SQ_MAX = (BOUND_MAX / SCALE) ** 2
BOUND_SLACK = 1.04
PE_DEN = 2
P_RING = 4


def project(nc, ctx, dram, args, banks, wf):
    x, Wq, Wk, Wv, Wf = args

    def sb(name, shape, dt):
        return ctx.enter_context(nc.sbuf_tensor(name, shape, dt))

    def sem(name):
        return ctx.enter_context(nc.semaphore(name))

    ident = sb("ident", [P, P], FP32)
    head_sum = sb("head_sum", [P, HD], BF16)
    w_in = sb("w_in", [P, 4, DC, D], FP32)
    w_hi = sb("w_hi", [P, 3, DC, D], FP32R)
    w_lo = sb("w_lo", [P, 3, DC, D], FP32R)
    x_in = sb("x_in", [P, TPB, D], FP32)
    xT_hi = sb("xT_hi", [P, DC, BLK], FP32R)
    xT_lo = sb("xT_lo", [P, DC, BLK], FP32R)
    qk_hi = sb("qk_hi", [P, 2 * NG, BLK], FP32R)
    qk_lo = sb("qk_lo", [P, 2 * NG, BLK], FP32R)
    v_out = sb("v_out", [P, TPB, D], FP32)
    squares = sb("squares", [P, 2, BLK], BF16)
    norms = sb("norms", [P, 2, NBLK], FP32)
    top = sb("top", [P, 2], FP32)
    top_both = sb("top_both", [1, 2], FP32)
    top_product = sb("top_product", [1, 1], FP32)
    ones_row = sb("ones_row", [1, P], FP32)
    bound_sq = sb("bound_sq", [P, 1], FP32)
    bound = sb("bound", [P, 1], FP32)
    flag = dram["flag"]
    shift_rows = sb("shift_rows", [N * H, S], FP32R)
    zero_rows = sb("zero_rows", [N * H, S], FP32)

    s_const = sem("s_const")
    s_hsum = sem("s_hsum")
    s_w = [sem(f"s_w{m}") for m in range(4)]
    s_sign = sem("s_sign")
    s_wT = sem("s_wT")
    s_whi = sem("s_whi")
    s_wdone = sem("s_wdone")
    s_x = sem("s_x")
    s_xT = sem("s_xT")
    s_xhi = sem("s_xhi")
    s_xlo = sem("s_xlo")
    s_prod = sem("s_prod")
    s_hi = sem("s_hi")
    s_sq = sem("s_sq")
    s_lo = sem("s_lo")
    s_norm = sem("s_norm")
    s_max = sem("s_max")
    s_qst, s_kst, s_vst = sem("s_qst"), sem("s_kst"), sem("s_vst")
    s_top = sem("s_top")
    s_topT = sem("s_topT")
    s_bound = sem("s_bound")
    s_shift = sem("s_shift")

    prod_bank = [banks[:, 2 + j, :] for j in range(4)]
    NP = 2 * NG + TPB

    block = ctx.enter_context(nc.Block())

    @block.sync
    def _(sp):
        for m, w in enumerate((Wq, Wk, Wv, Wf)):
            sp.dma_start(w_in[:, m], w.rearrange("(t p) i -> p t i", p=P)).then_inc(s_w[m], 16)
        sp.dma_start(x_in[:], x[0]).then_inc(s_x, 16)
        with sp.Fori(0, NBLK) as b:
            batch = sp.snap(b // QB)
            column = sp.snap((b % QB) * BLK)
            ahead = sp.snap((b + 1) % NBLK)
            sp.wait_ge(s_xT, b * DC + DC)
            sp.dma_start(x_in[:], x[bass.ds(ahead, 1)].rearrange("o p t d -> p (o t) d")).then_inc(s_x, 16)
            for first, hi, lo, store in ((0, "q_hi", "q_lo", s_qst), (NG, "k_hi", "k_lo", s_kst)):
                for part, src in ((hi, qk_hi), (lo, qk_lo)):
                    if first == 0:
                        sp.wait_ge(s_lo, b * 2 * NG + NG)
                    else:
                        sp.wait_ge(s_lo, b * 2 * NG + 2 * NG)
                    sp.dma_start(dram[part][bass.ds(batch, 1), :, bass.ds(column, BLK)]
                                 .rearrange("o (g p) t -> p (o g) t", p=P),
                                 src[:, first:first + NG, :].bitcast(FP32)).then_inc(store, 16)
            sp.wait_ge(s_hi, b * NP + NP + 1)
            sp.dma_start(dram["v"][bass.ds(b, 1)].rearrange("o (t p) d -> p (o t) d", p=P),
                         v_out[:]).then_inc(s_vst, 16)
        sp.wait_ge(s_qst, 32 * NBLK)
        sp.wait_ge(s_kst, 32 * NBLK)
        sp.wait_ge(s_vst, 16 * NBLK)
        sp.wait_ge(s_x, 16 * (NBLK + 1))
        sp.wait_ge(s_top, 7)
        sp.dma_start(dram["shift"][0], shift_rows[:].bitcast(FP32)).then_inc(s_shift, 16)
        sp.dma_start(dram["shift"][1], zero_rows[:]).then_inc(s_shift, 16)
        sp.wait_ge(s_shift, 32)

    @block.gpsimd
    def _(pool):
        nc.gpsimd.memset(ident[:], 0.0).then_inc(s_const, 1)
        nc.gpsimd.memset(head_sum[:], 0.0).then_inc(s_const, 1)
        nc.gpsimd.memset(ones_row[:], 1.0).then_inc(s_const, 1)
        nc.gpsimd.memset(zero_rows[:], 0.0).then_inc(s_const, 1)
        pool.wait_ge(s_const, 4)
        nc.gpsimd.affine_select(out=ident[:], in_=ident[:], compare_op=ALU.not_equal, fill=1.0, base=0,
                                pattern=[[-1, P]], channel_multiplier=1).then_inc(s_const, 1)
        for h in range(G):
            pool.wait_ge(s_const, 5)
            if h > 0:
                pool.wait_ge(s_hsum, h)
            cols = head_sum[HD * h:HD * h + HD, :].rearrange("p (r h) -> p h r", h=G)[:, h, :]
            nc.gpsimd.memset(cols, 1.0).then_inc(s_hsum, 1)

    @block.tensor
    def _(pe):
        pe.wait_ge(s_const, 5)
        for u in range(4 * DC):
            m, c = divmod(u, DC)
            if m < 3:
                pe.wait_ge(s_w[m], 16)
            else:
                pe.wait_ge(s_sign, 1)
            if u >= 2:
                pe.wait_ge(s_wdone, u - 1)
            for t in range(DC):
                last = nc.tensor.transpose(banks[:, u % 2, t * P:(t + 1) * P], w_in[:, m, t, c * P:(c + 1) * P], ident[:])
            last.then_inc(s_wT, 1)
        pe.wait_ge(s_wdone, 4 * DC)
        pe.wait_ge(s_hsum, G)

        def norm(j, b):
            pe.wait_ge(s_sq, b * 2 * NG + j + 1)
            if j == 0:
                pe.wait_ge(s_max, b * 2 + 1)
            mm = nc.tensor.matmul(banks[HD * (j % NG):HD * (j % NG) + HD, 6 + j // NG, :], head_sum[:], squares[:, j % 2, :],
                                  start=True, stop=True)
            mm.then_inc(s_norm, 1)

        with pe.Fori(0, NBLK) as b:
            pe.wait_ge(s_x, b * 16 + 16)
            for c in range(DC):
                pe.wait_ge(s_xlo, b * DC + c + 1)
                for t in range(TPB):
                    last = nc.tensor.transpose(banks[:, c % 2, t * P:(t + 1) * P], x_in[:, t, c * P:(c + 1) * P], ident[:])
                last.then_inc(s_xT, 1)
            pe.wait_ge(s_xlo, b * DC + DC + 2)
            for j in range(NP):
                if j < 4:
                    pe.wait_ge(s_hi, b * NP + 1)
                elif j < 2 * NG + 4:
                    pe.wait_ge(s_lo, b * 2 * NG + j - 3)
                pairs = []
                for c in range(DC):
                    if j < 2 * NG:
                        m, g = divmod(j, NG)
                        cols = slice(g * P, (g + 1) * P)
                        pairs += [(w_hi[:, m, c, cols], xT_hi[:, c, :]), (w_hi[:, m, c, cols], xT_lo[:, c, :]),
                                  (w_lo[:, m, c, cols], xT_hi[:, c, :])]
                    else:
                        cols = slice((j - 2 * NG) * P, (j - 2 * NG + 1) * P)
                        pairs += [(xT_hi[:, c, cols], w_hi[:, 2, c, :]), (xT_hi[:, c, cols], w_lo[:, 2, c, :]),
                                  (xT_lo[:, c, cols], w_hi[:, 2, c, :])]
                for i, (lhsT, rhs) in enumerate(pairs):
                    last = nc.tensor.matmul(prod_bank[j % 4], lhsT, rhs, start=(i == 0), stop=(i == len(pairs) - 1))
                last.then_inc(s_prod, 1)
                if 2 <= j < 2 * NG + 2:
                    norm(j - 2, b)
        pe.wait_ge(s_top, 1)
        for i in range(2):
            last = nc.tensor.transpose(banks[0:1, 0, i * P:(i + 1) * P], top[:, i:i + 1], ident[:])
        last.then_inc(s_topT, 1)
        pe.wait_ge(s_top, 3)
        nc.tensor.matmul(banks[:, 1, 0:1], ones_row[:], top_product[:], start=True, stop=True).then_inc(s_topT, 1)

    @block.scalar
    def _(act):
        act.sem_inc(s_hi, 1)
        for u in range(3 * DC):
            m, c = divmod(u, DC)
            act.wait_ge(s_wT, u + 1)
            nc.scalar.activation(w_hi[:, m, c, :], banks[:, u % 2, :], ACT.Copy).then_inc(s_whi, 1)
        with act.Fori(0, NBLK) as b:
            for c in range(DC):
                act.wait_ge(s_xT, b * DC + c + 1)
                nc.scalar.activation(xT_hi[:, c, :], banks[:, c % 2, :], ACT.Copy).then_inc(s_xhi, 1)
            for j in range(NP):
                act.wait_ge(s_prod, b * NP + j + 1)
                if j < 2 * NG:
                    if j == 0:
                        act.wait_ge(s_qst, b * 32 + 32)
                    if j == NG:
                        act.wait_ge(s_kst, b * 32 + 32)
                    nc.scalar.activation(qk_hi[:, j, :], prod_bank[j % 4], ACT.Copy).then_inc(s_hi, 1)
                    act.wait_ge(s_norm, b * 2 * NG + j + 1)
                    act.wait_ge(s_hi, b * NP + j + 2)
                    nc.scalar.activation(squares[:, j % 2, :], qk_hi[:, j, :].bitcast(FP32), ACT.Square).then_inc(s_sq, 1)
                else:
                    if j == 2 * NG:
                        act.wait_ge(s_vst, b * 16 + 16)
                    nc.scalar.activation(v_out[:, j - 2 * NG, :], prod_bank[j % 4], ACT.Copy).then_inc(s_hi, 1)
        act.wait_ge(s_top, 5)
        nc.scalar.activation(bound[:], bound_sq[:], ACT.Sqrt).then_inc(s_bound, 1)

    @block.vector
    def _(dve):
        dve.sem_inc(s_xlo, 2)
        dve.sem_inc(s_max, 1)
        dve.sem_inc(s_norm, 2)
        dve.sem_inc(s_qst, 32)
        dve.sem_inc(s_kst, 32)
        dve.sem_inc(s_vst, 16)
        dve.wait_ge(s_w[3], 16)
        nc.vector.tensor_scalar(w_in[:, 3], w_in[:, 3], 0.0, 2.0, ALU.is_ge, ALU.mult).then_inc(s_sign, 1)
        for u in range(4 * DC):
            m, c = divmod(u, DC)
            if m < 3:
                dve.wait_ge(s_whi, u + 1)
                nc.vector.tensor_tensor(w_lo[:, m, c, :], banks[:, u % 2, :], w_hi[:, m, c, :].bitcast(FP32),
                                        ALU.subtract).then_inc(s_wdone, 1)
            else:
                dve.wait_ge(s_wT, u + 1)
                nc.vector.tensor_scalar(wf[:, c, :], banks[:, u % 2, :], -1.0, None, ALU.add).then_inc(s_wdone, 1)
        with dve.Fori(0, NBLK) as b:
            for c in range(DC):
                dve.wait_ge(s_xhi, b * DC + c + 1)
                nc.vector.tensor_tensor(xT_lo[:, c, :], banks[:, c % 2, :], xT_hi[:, c, :].bitcast(FP32),
                                        ALU.subtract).then_inc(s_xlo, 1)
            for j in range(2 * NG):
                dve.wait_ge(s_hi, b * NP + j + 2)
                nc.vector.tensor_tensor(qk_lo[:, j, :], prod_bank[j % 4], qk_hi[:, j, :].bitcast(FP32),
                                        ALU.subtract).then_inc(s_lo, 1)
            for half in range(2):
                dve.wait_ge(s_norm, b * 2 * NG + (half + 1) * NG + 2)
                nc.vector.reduce_max(norms[:, half, bass.ds(b, 1)], banks[:, 6 + half, :], AX.X).then_inc(s_max, 1)
        dve.wait_ge(s_max, 2 * NBLK + 1)
        nc.vector.reduce_max(top[:], norms[:], AX.X).then_inc(s_top, 1)
        dve.wait_ge(s_topT, 1)
        nc.vector.reduce_max(top_both[:], banks[0:1, 0, 0:2 * P].rearrange("o (i p) -> o i p", i=2), AX.X).then_inc(s_top, 1)
        dve.wait_ge(s_top, 2)
        nc.vector.tensor_tensor(top_product[:], top_both[:, 0:1], top_both[:, 1:2], ALU.mult).then_inc(s_top, 1)
        dve.wait_ge(s_topT, 2)
        nc.vector.tensor_scalar(flag[:], banks[0:1, 1, 0:1], BOUND_SLACK, BOUND_SQ_MAX, ALU.mult, ALU.is_gt).then_inc(s_top, 1)
        nc.vector.tensor_scalar(bound_sq[:], banks[:, 1, 0:1], BOUND_SLACK, BOUND_SQ_MAX, ALU.mult, ALU.min).then_inc(s_top, 1)
        dve.wait_ge(s_bound, 1)
        nc.vector.tensor_scalar(bound[:], bound[:], -SHIFT, None, ALU.mult).then_inc(s_top, 1)
        dve.wait_ge(s_top, 6)
        dve.wait_ge(s_const, 5)
        nc.vector.tensor_scalar(shift_rows[:], zero_rows[:], bound[0:N * H, :], None, ALU.add).then_inc(s_top, 1)


def exact_maxima(nc, ctx, dram, banks):

    def sb(name, shape, dt):
        return ctx.enter_context(nc.sbuf_tensor(name, shape, dt))

    def sem(name):
        return ctx.enter_context(nc.semaphore(name))

    q_head = sb("q_head", [3 * HD, S], FP32R)
    k_head = sb("k_head", [3 * HD, S], FP32R)
    maxima = sb("maxima", [P, KT], FP32)
    max_hi = sb("max_hi", [KT, P], FP32R)
    max_lo = sb("max_lo", [KT, P], FP32R)
    ident2 = sb("ident2", [P, P], FP32)
    flag = dram["flag"]

    m_id = sem("m_id")
    m_load = sem("m_load")
    m_score = sem("m_score")
    m_max = sem("m_max")
    m_T = sem("m_T")
    m_hi = sem("m_hi")
    m_lo = sem("m_lo")
    m_store = sem("m_store")

    block = ctx.enter_context(nc.Block())

    @block.sync
    def _(sp):
        needed = sp.value_load(flag[0:1, 0:1])
        with sp.If(needed > 0):
            with sp.Fori(0, N * H) as h:
                sp.wait_ge(m_store, h * 32 + 32)
                for r, (qs, ks) in enumerate((("q_hi", "k_hi"), ("q_lo", "k_hi"), ("q_hi", "k_lo"))):
                    for dst, src in ((q_head, qs), (k_head, ks)):
                        rows = dram[src].rearrange("n (h r) t -> (n h) r t", r=HD)[bass.ds(h, 1)]
                        sp.dma_start(dst[HD * r:HD * r + HD, :].bitcast(FP32), rows.rearrange("o r t -> (o r) t")).then_inc(m_load, 16)
                sp.wait_ge(m_lo, h + 2)
                for part, src in ((0, max_hi), (1, max_lo)):
                    row = dram["shift"][part][bass.ds(h, 1)].rearrange("o (t p) -> (o t) p", p=P)
                    sp.dma_start(row, src[:].bitcast(FP32)).then_inc(m_store, 16)
            sp.wait_ge(m_store, 32 * N * H + 32)

    @block.gpsimd
    def _(pool):
        nc.gpsimd.memset(ident2[:], 0.0).then_inc(m_id, 1)
        pool.wait_ge(m_id, 1)
        nc.gpsimd.affine_select(out=ident2[:], in_=ident2[:], compare_op=ALU.not_equal, fill=1.0, base=0,
                                pattern=[[-1, P]], channel_multiplier=1).then_inc(m_id, 1)
        pool.sem_inc(m_store, 32)
        pool.sem_inc(m_max, 2)
        pool.sem_inc(m_lo, 1)

    @block.tensor
    def _(pe):
        needed = pe.value_load(flag[0:1, 0:1])
        with pe.If(needed > 0):
            pe.wait_ge(m_id, 2)
            with pe.Fori(0, N * H) as h:
                pe.wait_ge(m_load, h * 96 + 96)
                for t in range(KT):
                    pe.wait_ge(m_max, h * KT + t + 1)
                    if t == 0:
                        pe.wait_ge(m_lo, h + 1)
                    for kb in range(QB):
                        last = nc.tensor.matmul(banks[:, 4 * (t % 2) + kb, :], q_head[:, t * P:(t + 1) * P],
                                                k_head[:, kb * BLK:(kb + 1) * BLK], start=True, stop=True)
                    last.then_inc(m_score, 1)
                pe.wait_ge(m_max, h * KT + KT + 2)
                nc.tensor.transpose(banks[0:KT, 0, 0:P], maxima[:], ident2[:]).then_inc(m_T, 1)

    @block.vector
    def _(dve):
        needed = dve.value_load(flag[0:1, 0:1])
        with dve.If(needed > 0):
            with dve.Fori(0, N * H) as h:
                for t in range(KT):
                    dve.wait_ge(m_score, h * KT + t + 1)
                    nc.vector.reduce_max(maxima[:, t:t + 1], banks[:, 4 * (t % 2):4 * (t % 2) + 4, :]
                                         .rearrange("p b k -> p (b k)"), AX.X).then_inc(m_max, 1)
                dve.wait_ge(m_T, h + 1)
                dve.wait_ge(m_store, h * 32 + 32)
                nc.vector.tensor_scalar(max_hi[:], banks[0:KT, 0, 0:P], -1.0, None, ALU.mult).then_inc(m_hi, 1)
                dve.wait_ge(m_hi, h + 1)
                nc.vector.scalar_tensor_tensor(out=max_lo[:], in0=banks[0:KT, 0, 0:P], scalar=-1.0, in1=max_hi[:].bitcast(FP32),
                                               op0=ALU.mult, op1=ALU.subtract).then_inc(m_lo, 1)


def attend(nc, ctx, dram, banks):

    def sb(name, shape, dt):
        return ctx.enter_context(nc.sbuf_tensor(name, shape, dt))

    def sem(name):
        return ctx.enter_context(nc.semaphore(name))

    q_rows = sb("q_rows", [KROWS, G, S], FP32R)
    k_rows = sb("k_rows", [KROWS, G, S], FP32R)
    v_keys = sb("v_keys", [P, KT, P], FP32)
    probs = sb("probs", [P, P_RING, G, BLK], FP32)
    sums = sb("sums", [P, 2, G, BLK], FP32)
    ones = sb("ones", [P, HD], FP32)
    out_sb = sb("out_sb", [P, 2, BLK], FP32)
    den_sb = sb("den_sb", [P, 2, BLK], FP32)

    a_one = sem("a_one")
    a_q = [sem(f"a_q{c}") for c in range(QB)]
    a_k = [sem(f"a_k{c}") for c in range(QB)]
    a_score = [sem(f"a_score{h}") for h in range(2)]
    a_prob = [sem(f"a_prob{h}") for h in range(2)]
    a_pv = sem("a_pv")
    a_sum = [sem(f"a_sum{h}") for h in range(2)]
    a_den = sem("a_den")
    a_out = sem("a_out")
    a_dout = sem("a_dout")
    a_store = [sem(f"a_store{h}") for h in range(2)]

    NV = KT - PE_DEN
    STEP_Q = 4 * 16
    STEP_K = 4 * 16

    def load_q(sp, it, c):
        cols = slice(c * BLK, (c + 1) * BLK)
        for r, part in enumerate(("q_hi", "q_lo", "q_hi")):
            src = dram[part].rearrange("n (g h r) t -> (n g) r h t", g=NG, r=HD)[bass.ds(it, 1), :, :, cols]
            sp.dma_start(q_rows[HD * r:HD * r + HD, :, cols].bitcast(FP32), src.rearrange("o r h t -> (o r) h t")).then_inc(a_q[c], 16)
        src = dram["shift"].rearrange("s (i h) t -> i s h t", h=G)[bass.ds(it, 1), :, :, cols]
        sp.dma_start(q_rows[3 * HD:KROWS, :, cols].bitcast(FP32), src.rearrange("o s h t -> (o s) h t")).then_inc(a_q[c], 16)

    def load_k(sp, it, c):
        cols = slice(c * BLK, (c + 1) * BLK)
        for r, part in enumerate(("k_hi", "k_hi", "k_lo")):
            src = dram[part].rearrange("n (g h r) t -> (n g) r h t", g=NG, r=HD)[bass.ds(it, 1), :, :, cols]
            sp.dma_start(k_rows[HD * r:HD * r + HD, :, cols].bitcast(FP32), src.rearrange("o r h t -> (o r) h t")).then_inc(a_k[c], 16)

    block = ctx.enter_context(nc.Block())

    @block.sync
    def _(sp):
        v_src = dram["v"].rearrange("(n b) (t p) (g d) -> n g b p t d", n=N, p=P, g=NG)

        def load_v(n, g, c):
            src = v_src[bass.ds(n, 1), bass.ds(g, 1), c].rearrange("o u p t d -> p (o u t) d")
            sp.dma_start(v_keys[:, c * TPB:(c + 1) * TPB, :], src).then_inc(a_k[c], 16)

        def store(it, qb):
            cols = slice(qb * BLK, (qb + 1) * BLK)
            sp.wait_ge(a_out, it * QB + qb + 1 + 2)
            dst = dram["attn"].rearrange("n (g p) t -> (n g) p t", p=P)[bass.ds(it, 1), :, cols]
            sp.dma_start(dst.rearrange("o p t -> (o p) t"), out_sb[:, qb % 2, :]).then_inc(a_store[qb % 2], 16)
            sp.wait_ge(a_dout, it * QB + qb + 1 + 2)
            dst = dram["den"].rearrange("(i h) t -> i h t", h=G)[bass.ds(it, 1), :, cols]
            sp.dma_start(dst.rearrange("o h t -> (o h) t"), den_sb[0:P:HD, qb % 2, :]).then_inc(a_store[qb % 2], 16)

        for c in range(QB):
            load_q(sp, 0, c)
            load_k(sp, 0, c)
            load_v(0, 0, c)
        with sp.Fori(0, ITEMS - 1) as it:
            ahead = sp.snap(it + 1)
            n_ahead = sp.snap((it + 1) // NG)
            g_ahead = sp.snap((it + 1) % NG)
            for qb in range(QB):
                if qb == QB - 1:
                    for c in range(QB):
                        for h in range(2):
                            sp.wait_ge(a_score[h], it * (QB * KT) + (QB - 1) * KT + (c + 1) * TPB)
                        load_k(sp, ahead, c)
                        sp.wait_ge(a_pv, it * (QB * KT) + (QB - 1) * KT + (c + 1) * TPB + P_RING)
                        load_v(n_ahead, g_ahead, c)
                for h in range(2):
                    sp.wait_ge(a_score[h], it * (QB * KT) + (qb + 1) * KT)
                load_q(sp, ahead, qb)
                store(it, qb)
        for qb in range(QB):
            store(ITEMS - 1, qb)
        for h in range(2):
            sp.wait_ge(a_store[h], ITEMS * QB // 2 * 32 + 32)

    @block.gpsimd
    def _(pool):
        nc.gpsimd.memset(ones[:], 1.0).then_inc(a_one, 1)
        pool.wait_ge(a_one, 1)
        nc.gpsimd.memset(k_rows[3 * HD:KROWS, :, :].bitcast(FP32), 1.0).then_inc(a_one, 1)

    @block.tensor
    def _(pe):
        pe.sem_inc(a_pv, P_RING)
        pe.sem_inc(a_den, 2)
        pe.wait_ge(a_one, 2)
        with pe.Fori(0, ITEMS) as it:

            def scores(qb, kt):
                if kt == 0:
                    pe.wait_ge(a_q[qb], it * STEP_Q + STEP_Q)
                if qb == 0 and kt % TPB == 0:
                    pe.wait_ge(a_k[kt // TPB], it * STEP_K + STEP_K)
                for half in range(2):
                    pe.wait_ge(a_prob[half], it * (QB * KT) + qb * KT + kt + 1)
                    for h in (2 * half, 2 * half + 1):
                        last = nc.tensor.matmul(banks[:, h, :], k_rows[:, h, kt * P:(kt + 1) * P],
                                                q_rows[:, h, qb * BLK:(qb + 1) * BLK], start=True, stop=True)
                    last.then_inc(a_score[half], 1)

            def values(qb, kt):
                for half in range(2):
                    pe.wait_ge(a_prob[half], it * (QB * KT) + qb * KT + kt + 2)
                if kt == 0:
                    pe.wait_ge(a_out, it * QB + qb + 1)
                for h in range(G):
                    rows = slice(HD * h, HD * h + HD)
                    last = nc.tensor.matmul(banks[rows, 4 + qb % 2, :], v_keys[:, kt, rows], probs[:, kt % P_RING, h, :],
                                            start=(kt == 0), stop=(kt == KT - 1))
                if kt >= NV:
                    if kt == NV:
                        pe.wait_ge(a_dout, it * QB + qb + 1)
                    for h in range(G):
                        rows = slice(HD * h, HD * h + HD)
                        last = nc.tensor.matmul(banks[rows, 6 + qb % 2, :], ones[:], probs[:, kt % P_RING, h, :],
                                                start=(kt == NV), stop=False)
                last.then_inc(a_pv, 1)

            def denominators(qb):
                for half in range(2):
                    pe.wait_ge(a_sum[half], it * (QB * NV) + (qb + 1) * NV + 1)
                for h in range(G):
                    rows = slice(HD * h, HD * h + HD)
                    last = nc.tensor.matmul(banks[rows, 6 + qb % 2, :], ones[:], sums[:, qb % 2, h, :], start=False, stop=True)
                last.then_inc(a_den, 1)

            for qb in range(QB):
                for kt in range(KT):
                    scores(qb, kt)
                    if kt > 0:
                        values(qb, kt - 1)
                    elif qb > 0:
                        values(qb - 1, KT - 1)
                        denominators(qb - 1)
            values(QB - 1, KT - 1)
            denominators(QB - 1)

    @block.scalar
    def _(act):
        act.sem_inc(a_prob[0], 1)
        act.sem_inc(a_prob[1], 1)
        act.sem_inc(a_out, 2)
        with act.Fori(0, ITEMS) as it:

            def copy_out(qb):
                act.wait_ge(a_den, it * QB + qb + 1 + 2)
                act.wait_ge(a_store[qb % 2], it * QB * 16 + qb // 2 * 32 + 32)
                nc.scalar.activation(out_sb[:, qb % 2, :], banks[:, 4 + qb % 2, :], ACT.Copy).then_inc(a_out, 1)

            for qb in range(QB):
                for kt in range(KT):
                    for half in range(2):
                        act.wait_ge(a_score[half], it * (QB * KT) + qb * KT + kt + 1)
                        if half == 0:
                            act.wait_ge(a_pv, it * (QB * KT) + qb * KT + kt + 1)
                        if kt >= P_RING:
                            act.wait_ge(a_sum[half], it * (QB * NV) + qb * NV + min(kt - P_RING + 1, NV) + 1)
                        else:
                            act.wait_ge(a_sum[half], it * (QB * NV) + qb * NV + 1)
                        heads = slice(2 * half, 2 * half + 2)
                        nc.scalar.activation(probs[:, kt % P_RING, heads, :], banks[:, heads, :], ACT.Exp,
                                             scale=SCALE).then_inc(a_prob[half], 1)
                    if qb > 0 and kt == 3:
                        copy_out(qb - 1)
            copy_out(QB - 1)

    @block.vector
    def _(dve):
        dve.sem_inc(a_sum[0], 1)
        dve.sem_inc(a_sum[1], 1)
        dve.sem_inc(a_dout, 2)
        dve.sem_inc(a_store[0], 32)
        dve.sem_inc(a_store[1], 32)
        with dve.Fori(0, ITEMS) as it:

            def copy_den(qb):
                dve.wait_ge(a_den, it * QB + qb + 1 + 2)
                dve.wait_ge(a_store[qb % 2], it * QB * 16 + qb // 2 * 32 + 32)
                nc.vector.tensor_copy(den_sb[:, qb % 2, :], banks[:, 6 + qb % 2, :]).then_inc(a_dout, 1)

            for qb in range(QB):
                for kt in range(1, NV):
                    for half in range(2):
                        heads = slice(2 * half, 2 * half + 2)
                        dve.wait_ge(a_prob[half], it * (QB * KT) + qb * KT + kt + 2)
                        total = sums[:, qb % 2, heads, :]
                        if kt == 1:
                            dve.wait_ge(a_den, it * QB + qb + 1)
                            nc.vector.tensor_tensor(total, probs[:, 0, heads, :], probs[:, 1, heads, :], ALU.add).then_inc(a_sum[half], 2)
                        else:
                            dve.wait_ge(a_sum[half], it * (QB * NV) + qb * NV + kt + 1)
                            nc.vector.tensor_tensor(total, total, probs[:, kt % P_RING, heads, :], ALU.add).then_inc(a_sum[half], 1)
                    if qb > 0 and kt == 3:
                        copy_den(qb - 1)
            copy_den(QB - 1)


def normalise_and_ffn(nc, ctx, dram, args, banks, wf, out):
    x, scale, bias = args

    def sb(name, shape, dt):
        return ctx.enter_context(nc.sbuf_tensor(name, shape, dt))

    def sem(name):
        return ctx.enter_context(nc.semaphore(name))

    T = QB * TPB
    ident3 = sb("ident3", [P, P], FP32)
    scale_b = sb("scale_b", [P, D], FP32)
    bias_b = sb("bias_b", [P, D], FP32)
    eps = sb("eps", [P, 1], FP32)
    x_in = sb("x_res", [P, 2, TPB, D], FP32)
    attnT = sb("attnT", [P, 2, DC, BLK], FP32)
    den_in = sb("den_in", [H, 2, BLK], FP32)
    rden = sb("rden", [P, 2, H], FP32)
    attn = sb("attn", [P, 2, D], FP32)
    res1 = sb("res1", [P, 2, D], FP32)
    y = sb("y", [P, 2, D], FP32)
    yT_hi = sb("yT_hi", [P, 2, D], FP32R)
    yT_lo = sb("yT_lo", [P, 2, D], FP32R)
    z = sb("z", [P, 2, D], FP32)
    zb = sb("zb", [P, 2, D], FP32)
    zc = sb("zc", [P, 2, D], FP32)
    res2 = sb("res2", [P, 2, D], FP32)
    y2 = sb("y2", [P, 2, D], FP32)
    stats = sb("stats", [P, 2, 2, 6], FP32)
    mean_var = sb("mean_var", [P, 2, 2, 2], FP32)
    std = sb("std", [P, 2, 2, 1], FP32)
    rstd = sb("rstd", [P, 2, 2, 1], FP32)

    f_const = sem("f_const")
    f_in = [sem(f"f_in{k}") for k in range(2)]
    f_aT = sem("f_aT")
    f_rden = sem("f_rden")
    f_attn = sem("f_attn")
    f_res = [sem("f_res1"), sem("f_res2")]
    f_stat = [sem("f_stat1"), sem("f_stat2")]
    f_order = sem("f_order")
    f_std = [sem("f_std1"), sem("f_std2")]
    f_rstd = [sem("f_rstd1"), sem("f_rstd2")]
    f_y = [sem("f_y1"), sem("f_y2")]
    f_yT = sem("f_yT")
    f_yhi = sem("f_yhi")
    f_ylo = sem("f_ylo")
    f_ffn = sem("f_ffn")
    f_z = sem("f_z")
    f_zb = sem("f_zb")
    f_zc = sem("f_zc")
    f_out = [sem(f"f_out{k}") for k in range(2)]

    def aT_bank(t):
        return banks[:, t % 2, :]

    def den_bank(t):
        return banks[:, 6 + t % 2, 0:H]

    def yT_bank(t):
        return banks[:, 2 + t % 2, :]

    def ffn_bank(t):
        return banks[:, 4 + t % 2, :]

    block = ctx.enter_context(nc.Block())

    @block.sync
    def _(sp):
        sp.dma_start(scale_b[:], scale.partition_broadcast(P)).then_inc(f_const, 16)
        sp.dma_start(bias_b[:], bias.partition_broadcast(P)).then_inc(f_const, 16)
        with sp.Fori(0, N) as n:
            for qb in range(QB):
                blk = sp.snap(n * QB + qb)
                cols = slice(qb * BLK, (qb + 1) * BLK)
                k = qb % 2
                sp.wait_ge(f_res[0], n * T + qb * TPB + TPB)
                sp.dma_start(x_in[:, k], x[bass.ds(blk, 1)].rearrange("o p t d -> p (o t) d")).then_inc(f_in[k], 16)
                src = dram["attn"][bass.ds(n, 1), :, cols].rearrange("o (c p) t -> p (o c) t", p=P)
                sp.dma_start(attnT[:, k], src).then_inc(f_in[k], 16)
                src = dram["den"].rearrange("(n h) t -> n h t", n=N)[bass.ds(n, 1), :, cols]
                sp.dma_start(den_in[:, k], src.rearrange("o h t -> (o h) t")).then_inc(f_in[k], 16)

    @block.gpsimd
    def _(pool):
        nc.gpsimd.memset(ident3[:], 0.0).then_inc(f_const, 1)
        nc.gpsimd.memset(eps[:], EPS).then_inc(f_const, 1)
        pool.sem_inc(f_res[0], 2 * TPB)
        pool.sem_inc(f_res[1], 2)
        pool.sem_inc(f_zb, 2)
        pool.wait_ge(f_const, 34)
        nc.gpsimd.affine_select(out=ident3[:], in_=ident3[:], compare_op=ALU.not_equal, fill=1.0, base=0,
                                pattern=[[-1, P]], channel_multiplier=1).then_inc(f_const, 1)
        with pool.Fori(0, N) as n:
            for i in range(T + 2):
                t = i
                if t < T:
                    pool.wait_ge(f_attn, n * T + t + 1 + 2)
                    pool.wait_ge(f_y[0], n * T + t + 1)
                    nc.gpsimd.tensor_tensor(res1[:, t % 2], attn[:, t % 2], x_in[:, t // TPB % 2, t % TPB], ALU.add).then_inc(f_res[0], 1)
                t = i - 2
                if t >= 0:
                    pool.wait_ge(f_z, n * T + t + 1 + 2)
                    pool.wait_ge(f_zc, n * T + t + 1)
                    nc.gpsimd.tensor_tensor(zb[:, t % 2], z[:, t % 2], bias_b[:], ALU.add).then_inc(f_zb, 1)
                    pool.wait_ge(f_zc, n * T + t + 1 + 2)
                    pool.wait_ge(f_y[1], n * T + t + 1)
                    nc.gpsimd.tensor_tensor(res2[:, t % 2], zc[:, t % 2], y[:, t % 2], ALU.add).then_inc(f_res[1], 1)

    @block.tensor
    def _(pe):
        pe.sem_inc(f_ffn, 2)
        pe.wait_ge(f_const, 35)
        with pe.Fori(0, N) as n:
            for i in range(T + 2):
                t = i
                if t < T:
                    k = t // TPB % 2
                    cols = slice(t % TPB * P, (t % TPB + 1) * P)
                    if t % TPB == 0:
                        pe.wait_ge(f_in[k], n * (QB // 2 * 48) + t // TPB // 2 * 48 + 48)
                    pe.wait_ge(f_attn, n * T + t + 1)
                    for c in range(DC):
                        nc.tensor.transpose(aT_bank(t)[:, c * P:(c + 1) * P], attnT[:, k, c, cols], ident3[:])
                    nc.tensor.transpose(den_bank(t), den_in[:, k, cols], ident3[0:H, 0:H]).then_inc(f_aT, 1)
                t = i - 1
                if 0 <= t < T:
                    pe.wait_ge(f_y[0], n * T + t + 1 + 2)
                    pe.wait_ge(f_ylo, n * T + t + 1)
                    for c in range(DC):
                        last = nc.tensor.transpose(yT_bank(t)[:, c * P:(c + 1) * P], y[:, t % 2, c * P:(c + 1) * P], ident3[:])
                    last.then_inc(f_yT, 1)
                t = i - 2
                if t >= 0:
                    pe.wait_ge(f_ylo, n * T + t + 1 + 2)
                    pe.wait_ge(f_z, n * T + t + 1)
                    for c in range(DC):
                        for part in (yT_hi, yT_lo):
                            last = nc.tensor.matmul(ffn_bank(t), part[:, t % 2, c * P:(c + 1) * P], wf[:, c, :],
                                                    start=(c == 0 and part is yT_hi), stop=(c == DC - 1 and part is yT_lo))
                    last.then_inc(f_ffn, 1)

    @block.scalar
    def _(act):
        act.sem_inc(f_y[0], 2)
        act.sem_inc(f_y[1], 2)

        def deviation(n, t, which):
            act.wait_ge(f_stat[which], (n * T + t + 1) * 2)
            act.wait_ge(f_rstd[which], n * T + t + 1)
            nc.scalar.activation(std[:, t % 2, which], mean_var[:, t % 2, which, 1:2], ACT.Sqrt, bias=eps[:]).then_inc(f_std[which], 1)

        act.wait_ge(f_const, 34)
        with act.Fori(0, N) as n:
            for i in range(T + 2):
                t = i - 1
                if 0 <= t < T:
                    act.wait_ge(f_yT, n * T + t + 1)
                    act.wait_ge(f_ffn, n * T + t + 1)
                    nc.scalar.activation(yT_hi[:, t % 2], yT_bank(t), ACT.Copy).then_inc(f_yhi, 1)
                t = i
                if t < T:
                    deviation(n, t, 0)
                t = i - 2
                if t >= 0:
                    deviation(n, t, 1)
                    act.wait_ge(f_y[1], n * T + t + 1 + 2)
                    row = act.snap(n * T + t)
                    act.dma_start(out[bass.ds(row, 1)].rearrange("o p d -> (o p) d"), y2[:, t % 2]).then_inc(f_out[t % 2], 16)
        for k in range(2):
            act.wait_ge(f_out[k], N * T // 2 * 16 + 16)

    @block.vector
    def _(dve):
        dve.sem_inc(f_attn, 2)
        dve.sem_inc(f_ylo, 2)
        dve.sem_inc(f_z, 2)
        dve.sem_inc(f_zc, 2)
        dve.sem_inc(f_rstd[0], 2)
        dve.sem_inc(f_rstd[1], 2)
        dve.sem_inc(f_out[0], 16)
        dve.sem_inc(f_out[1], 16)
        dve.wait_ge(f_const, 34)

        def statistics(n, t, which, src, credit):
            dve.wait_ge(f_res[which], n * T + t + 1 + credit)
            nc.vector.bn_stats(stats[:, t % 2, which], src[:, t % 2]).then_inc(f_stat[which], 1)
            dve.wait_ge(f_stat[which], (n * T + t) * 2 + 1)
            dve.wait_ge(f_y[which], n * T + t + 1)
            dve.sem_inc(f_order, 1)
            nc.vector.bn_aggr(mean_var[:, t % 2, which], stats[:, t % 2, which]).then_inc(f_stat[which], 1)

        def layernorm(n, t, which, src, dst):
            dve.wait_ge(f_std[which], n * T + t + 1)
            nc.vector.reciprocal(rstd[:, t % 2, which], std[:, t % 2, which]).then_inc(f_rstd[which], 1)
            dve.wait_ge(f_rstd[which], n * T + t + 1 + 2)
            nc.vector.tensor_scalar(dst[:, t % 2], src[:, t % 2], mean_var[:, t % 2, which, 0:1], rstd[:, t % 2, which],
                                    ALU.subtract, ALU.mult).then_inc(f_y[which], 1)

        with dve.Fori(0, N) as n:
            for i in range(T + 2):
                t = i
                if t < T:
                    dve.wait_ge(f_aT, n * T + t + 1)
                    dve.wait_ge(f_attn, n * T + t + 1)
                    nc.vector.reciprocal(rden[:, t % 2], den_bank(t)).then_inc(f_rden, 1)
                    dve.wait_ge(f_rden, n * T + t + 1)
                    dve.wait_ge(f_res[0], n * T + t + 1 + 2 * TPB - 2)
                    nc.vector.tensor_tensor(attn[:, t % 2].rearrange("p (h d) -> p h d", h=H),
                                            aT_bank(t).rearrange("p (h d) -> p h d", h=H),
                                            rden[:, t % 2].unsqueeze(2).to_broadcast([P, H, HD]), ALU.mult).then_inc(f_attn, 1)
                t = i - 1
                if 0 <= t < T:
                    dve.wait_ge(f_yhi, n * T + t + 1)
                    nc.vector.tensor_tensor(yT_lo[:, t % 2], yT_bank(t), yT_hi[:, t % 2].bitcast(FP32), ALU.subtract).then_inc(f_ylo, 1)
                t = i - 2
                if t >= 0:
                    dve.wait_ge(f_ffn, n * T + t + 1 + 2)
                    dve.wait_ge(f_zb, n * T + t + 1)
                    nc.vector.tensor_tensor(z[:, t % 2], ffn_bank(t), scale_b[:], ALU.mult).then_inc(f_z, 1)
                t = i
                if t < T:
                    statistics(n, t, 0, res1, 2 * TPB)
                t = i - 2
                if t >= 0:
                    dve.wait_ge(f_zb, n * T + t + 1 + 2)
                    dve.wait_ge(f_res[1], n * T + t + 1)
                    nc.vector.tensor_scalar(zc[:, t % 2], zb[:, t % 2], -MAX_VAL, MAX_VAL, ALU.max, ALU.min).then_inc(f_zc, 1)
                t = i
                if t < T:
                    dve.wait_ge(f_res[1], n * T + t + 1)
                    layernorm(n, t, 0, res1, y)
                t = i - 2
                if t >= 0:
                    statistics(n, t, 1, res2, 2)
                    dve.wait_ge(f_out[t % 2], n * (T // 2 * 16) + t // 2 * 16 + 16)
                    layernorm(n, t, 1, res2, y2)


def build(nc, x, Wq, Wk, Wv, Wf, scale, bias, out):
    def scratch(name, shape, dt):
        return nc.dram_tensor("scratch_" + name, shape, dt, kind="Internal").ap()

    x_blocks = x.rearrange("n (b t p) d -> (n b) p t d", p=P, t=TPB)
    out_tiles = out.rearrange("n (t p) d -> (n t) p d", p=P)
    dram = {k: scratch(k, (N, D, S), FP32) for k in ("q_hi", "q_lo", "k_hi", "k_lo")}
    dram["v"] = scratch("v", (NBLK, BLK, D), FP32)
    dram["shift"] = scratch("shift", (2, N * H, S), FP32)
    dram["attn"] = scratch("attn", (N, D, S), FP32)
    dram["den"] = scratch("den", (N * H, S), FP32)
    with ExitStack() as whole:
        banks = whole.enter_context(nc.psum_tensor("banks", [P, 8, BLK], FP32))
        wf = whole.enter_context(nc.sbuf_tensor("wf", [P, DC, D], FP32R))
        dram["flag"] = whole.enter_context(nc.sbuf_tensor("flag", [1, 1], INT32))
        with ExitStack() as ctx:
            project(nc, ctx, dram, (x_blocks, Wq, Wk, Wv, Wf), banks, wf)
        with ExitStack() as ctx:
            exact_maxima(nc, ctx, dram, banks)
        with ExitStack() as ctx:
            attend(nc, ctx, dram, banks)
        with ExitStack() as ctx:
            normalise_and_ffn(nc, ctx, dram, (x_blocks, scale, bias), banks, wf, out_tiles)


_INS = ["L0_attn_x", "L0_attn_Wq", "L0_attn_Wk", "L0_attn_Wv", "L0_ffn_weights", "L0_ffn_scale", "L0_ffn_bias"]


def kernel(**inputs):
    import numpy as np
    import concourse.bacc as bacc
    from concourse.bass_utils import run_bass_kernel_spmd

    nc = bacc.Bacc("TRN2", target_bir_lowering=False, num_devices=1)
    arrays, args = {}, []
    for name in _INS:
        a = np.ascontiguousarray(inputs[name])
        arrays[f"in_{name}"] = a
        args.append(nc.dram_tensor(f"in_{name}", a.shape, mybir.dt.from_np(a.dtype), kind="ExternalInput").ap())
    out = nc.dram_tensor("out_x", (N, S, D), FP32, kind="ExternalOutput").ap()
    build(nc, *args, out)
    r = run_bass_kernel_spmd(nc, [arrays], core_ids=[0])
    return r.results[0]["out_x"]
```

```python
import concourse.bass as bass
from concourse import mybir
from contextlib import ExitStack

FP32 = mybir.dt.float32
FP32R = mybir.dt.float32r
BF16 = mybir.dt.bfloat16
INT32 = mybir.dt.int32
ALU = mybir.AluOpType
ACT = mybir.ActivationFunctionType
AX = mybir.AxisListType

P = 128
N, S, D = 4, 2048, 512
H, HD = 16, 32
G = P // HD
NG = H // G
DC = D // P
BLK = 512
TPB = BLK // P
NBLK = N * S // BLK
QB = S // BLK
KT = S // P
ITEMS = N * NG
SCALE = float(HD) ** -0.5
EPS = 1e-5
MAX_VAL = 100.0
KROWS = 3 * HD + 2
SHIFT = 0.25
BOUND_MAX = 64.0
BOUND_SQ_MAX = (BOUND_MAX / SCALE) ** 2
BOUND_SLACK = 1.04
PE_DEN = 1
P_RING = 8
SLOTS = 3
LAG = 2
DEN_LAG = 4


def project(nc, ctx, dram, args, banks, ffn):
    x, Wq, Wk, Wv, Wf, scale, bias = args
    wf_hi, wf_lo, bias_ones, bias_rows = ffn

    def sb(name, shape, dt):
        return ctx.enter_context(nc.sbuf_tensor(name, shape, dt))

    def sem(name):
        return ctx.enter_context(nc.semaphore(name))

    ident = sb("ident", [P, P], FP32)
    head_sum = sb("head_sum", [P, HD], BF16)
    w_in = sb("w_in", [P, 4, DC, D], FP32)
    w_hi = sb("w_hi", [P, 3, DC, D], FP32R)
    w_lo = sb("w_lo", [P, 3, DC, D], FP32R)
    x_in = sb("x_in", [P, TPB, D], FP32)
    xT_hi = sb("xT_hi", [P, 2, DC, BLK], FP32R)
    xT_lo = sb("xT_lo", [P, 2, DC, BLK], FP32R)
    qk_hi = sb("qk_hi", [P, 2 * NG, BLK], FP32R)
    qk_lo = sb("qk_lo", [P, 2 * NG, BLK], FP32R)
    v_out = sb("v_out", [P, TPB, D], FP32)
    squares = sb("squares", [P, 2 * NG, BLK], BF16)
    norms = sb("norms", [P, 2, NBLK], FP32)
    top = sb("top", [P, 2], FP32)
    top_both = sb("top_both", [1, 2], FP32)
    top_product = sb("top_product", [1, 1], FP32)
    ones_row = sb("ones_row", [1, P], FP32)
    bound_sq = sb("bound_sq", [P, 1], FP32)
    bound = sb("bound", [P, 1], FP32)
    flag = dram["flag"]
    scale_b = sb("scale_b", [P, D], FP32)
    bias_in = sb("bias_in", [2 * HD, D], FP32)
    wf_scaled = sb("wf_scaled", [P, 2, D], FP32)
    shift_rows = sb("shift_rows", [N * H, BLK], FP32R)
    zero_rows = sb("zero_rows", [N * H, BLK], FP32)

    s_const = sem("s_const")
    s_hsum = sem("s_hsum")
    s_w = [sem(f"s_w{m}") for m in range(4)]
    s_sign = sem("s_sign")
    s_ffn = sem("s_ffn")
    s_bias = sem("s_bias")
    s_scaled = sem("s_scaled")
    s_wT = sem("s_wT")
    s_whi = sem("s_whi")
    s_wdone = sem("s_wdone")
    s_x = sem("s_x")
    s_xT = sem("s_xT")
    s_xhi = sem("s_xhi")
    s_xlo = sem("s_xlo")
    s_prod = sem("s_prod")
    s_hi = sem("s_hi")
    s_sq = sem("s_sq")
    s_lo = sem("s_lo")
    s_norm = sem("s_norm")
    s_max = sem("s_max")
    s_qst, s_kst, s_vst = sem("s_qst"), sem("s_kst"), sem("s_vst")
    s_top = sem("s_top")
    s_topT = sem("s_topT")
    s_bound = sem("s_bound")
    s_shift = sem("s_shift")

    prod_bank = [banks[:, 2 + j, :] for j in range(4)]
    NP = 2 * NG + TPB

    block = ctx.enter_context(nc.Block())

    @block.sync
    def _(sp):
        for m, w in enumerate((Wq, Wk, Wv, Wf)):
            sp.dma_start(w_in[:, m], w.rearrange("(t p) i -> p t i", p=P)).then_inc(s_w[m], 16)
        sp.dma_start(x_in[:], x[0]).then_inc(s_x, 16)
        sp.dma_start(scale_b[:], scale.partition_broadcast(P)).then_inc(s_ffn, 16)
        for row in (0, HD):
            sp.dma_start(bias_in[row:row + 1, :], bias.partition_broadcast(1)).then_inc(s_ffn, 16)
        with sp.Fori(0, NBLK) as b:
            batch = sp.snap(b // QB)
            column = sp.snap((b % QB) * BLK)
            ahead = sp.snap((b + 1) % NBLK)
            sp.wait_ge(s_xT, b * DC + DC)
            sp.dma_start(x_in[:], x[bass.ds(ahead, 1)].rearrange("o p t d -> p (o t) d")).then_inc(s_x, 16)
            for first, hi, lo, store in ((0, "q_hi", "q_lo", s_qst), (NG, "k_hi", "k_lo", s_kst)):
                for part, src in ((hi, qk_hi), (lo, qk_lo)):
                    if first == 0:
                        sp.wait_ge(s_lo, b * 2 * NG + NG)
                    else:
                        sp.wait_ge(s_lo, b * 2 * NG + 2 * NG)
                    sp.dma_start(dram[part][bass.ds(batch, 1), :, bass.ds(column, BLK)]
                                 .rearrange("o (g p) t -> p (o g) t", p=P),
                                 src[:, first:first + NG, :].bitcast(FP32)).then_inc(store, 16)
            sp.wait_ge(s_hi, b * NP + NP + 4)
            sp.dma_start(dram["v"][bass.ds(b, 1)].rearrange("o (t p) d -> p (o t) d", p=P),
                         v_out[:]).then_inc(s_vst, 16)
        sp.wait_ge(s_qst, 32 * NBLK)
        sp.wait_ge(s_kst, 32 * NBLK)
        sp.wait_ge(s_vst, 16 * NBLK)
        sp.wait_ge(s_x, 16 * (NBLK + 1))
        sp.wait_ge(s_top, 7)
        for c in range(S // BLK):
            columns = slice(c * BLK, (c + 1) * BLK)
            sp.dma_start(dram["shift"][0][:, columns], shift_rows[:].bitcast(FP32)).then_inc(s_shift, 16)
            sp.dma_start(dram["shift"][1][:, columns], zero_rows[:]).then_inc(s_shift, 16)
        sp.wait_ge(s_shift, 32 * (S // BLK))

    @block.gpsimd
    def _(pool):
        nc.gpsimd.memset(ident[:], 0.0).then_inc(s_const, 1)
        nc.gpsimd.memset(head_sum[:], 0.0).then_inc(s_const, 1)
        nc.gpsimd.memset(ones_row[:], 1.0).then_inc(s_const, 1)
        nc.gpsimd.memset(zero_rows[:], 0.0).then_inc(s_const, 1)
        pool.wait_ge(s_const, 4)
        nc.gpsimd.affine_select(out=ident[:], in_=ident[:], compare_op=ALU.not_equal, fill=1.0, base=0,
                                pattern=[[-1, P]], channel_multiplier=1).then_inc(s_const, 1)
        for h in range(G):
            pool.wait_ge(s_const, 5)
            if h > 0:
                pool.wait_ge(s_hsum, h)
            cols = head_sum[HD * h:HD * h + HD, :].rearrange("p (r h) -> p h r", h=G)[:, h, :]
            nc.gpsimd.memset(cols, 1.0).then_inc(s_hsum, 1)
        pool.wait_ge(s_hsum, G)
        nc.gpsimd.memset(bias_ones[:].bitcast(FP32), 1.0).then_inc(s_hsum, 1)
        pool.wait_ge(s_hsum, G + 1)
        nc.gpsimd.memset(bias_rows[:].bitcast(FP32), 0.0).then_inc(s_hsum, 2)

    @block.tensor
    def _(pe):
        pe.wait_ge(s_const, 5)
        for u in range(4 * DC):
            m, c = divmod(u, DC)
            if m < 3:
                pe.wait_ge(s_w[m], 16)
            else:
                pe.wait_ge(s_sign, 1)
            if u >= 2:
                pe.wait_ge(s_wdone, u - 1)
            for t in range(DC):
                last = nc.tensor.transpose(banks[:, u % 2, t * P:(t + 1) * P], w_in[:, m, t, c * P:(c + 1) * P], ident[:])
            last.then_inc(s_wT, 1)
        pe.wait_ge(s_wdone, 4 * DC)
        pe.wait_ge(s_hsum, G + 3)

        def transpose_x(b, par):
            pe.wait_ge(s_x, b * 16 + 16)
            for c in range(DC):
                pe.wait_ge(s_xlo, b * DC + c + 1)
                for t in range(TPB):
                    last = nc.tensor.transpose(banks[:, c % 2, t * P:(t + 1) * P], x_in[:, t, c * P:(c + 1) * P], ident[:])
                last.then_inc(s_xT, 1)

        def norms_of(half, b):
            pe.wait_ge(s_sq, b * 2 * NG + (half + 1) * NG)
            pe.wait_ge(s_max, b * 2 + half + 1)
            for g in range(NG):
                last = nc.tensor.matmul(banks[HD * g:HD * g + HD, 6 + half, :], head_sum[:], squares[:, half * NG + g, :],
                                        start=True, stop=True)
            last.then_inc(s_norm, 1)

        transpose_x(0, 0)
        with pe.Fori(0, NBLK // 2) as pair:
            for par in range(2):
                b = pair * 2 + par
                pe.wait_ge(s_xlo, b * DC + DC + 2)
                for j in range(NP):
                    if j < 4:
                        pe.wait_ge(s_hi, b * NP + j + 1)
                    else:
                        pe.wait_ge(s_lo, b * 2 * NG + j - 3)
                    for c in range(DC):
                        if j < 2 * NG:
                            m, g = divmod(j, NG)
                            cols = slice(g * P, (g + 1) * P)
                            parts = [(w_hi[:, m, c, cols], xT_hi[:, par, c, :]), (w_hi[:, m, c, cols], xT_lo[:, par, c, :]),
                                     (w_lo[:, m, c, cols], xT_hi[:, par, c, :])]
                        else:
                            cols = slice((j - 2 * NG) * P, (j - 2 * NG + 1) * P)
                            parts = [(xT_hi[:, par, c, cols], w_hi[:, 2, c, :]), (xT_hi[:, par, c, cols], w_lo[:, 2, c, :]),
                                     (xT_lo[:, par, c, cols], w_hi[:, 2, c, :])]
                        for i, (lhsT, rhs) in enumerate(parts):
                            last = nc.tensor.matmul(prod_bank[j % 4], lhsT, rhs, start=(c == 0 and i == 0),
                                                    stop=(c == DC - 1 and i == 2))
                    last.then_inc(s_prod, 1)
                    if j == NG + 1:
                        norms_of(0, b)
                    if j == NP - 3:
                        norms_of(1, b)
                    if j == NP - 2:
                        transpose_x(b + 1, 1 - par)
        pe.wait_ge(s_top, 1)
        for i in range(2):
            last = nc.tensor.transpose(banks[0:1, 0, i * P:(i + 1) * P], top[:, i:i + 1], ident[:])
        last.then_inc(s_topT, 1)
        pe.wait_ge(s_top, 3)
        nc.tensor.matmul(banks[:, 1, 0:1], ones_row[:], top_product[:], start=True, stop=True).then_inc(s_topT, 1)

    @block.scalar
    def _(act):
        act.sem_inc(s_hi, 4)
        for u in range(3 * DC):
            m, c = divmod(u, DC)
            act.wait_ge(s_wT, u + 1)
            nc.scalar.activation(w_hi[:, m, c, :], banks[:, u % 2, :], ACT.Copy).then_inc(s_whi, 1)
        def split_x(b, par):
            for c in range(DC):
                act.wait_ge(s_xT, b * DC + c + 1)
                nc.scalar.activation(xT_hi[:, par, c, :], banks[:, c % 2, :], ACT.Copy).then_inc(s_xhi, 1)

        split_x(0, 0)
        with act.Fori(0, NBLK // 2) as pair:
            for par in range(2):
                b = pair * 2 + par
                for j in range(NP):
                    act.wait_ge(s_prod, b * NP + j + 1)
                    if j < 2 * NG:
                        if j == 0:
                            act.wait_ge(s_qst, b * 32 + 32)
                        if j == NG:
                            act.wait_ge(s_kst, b * 32 + 32)
                        nc.scalar.activation(qk_hi[:, j, :], prod_bank[j % 4], ACT.Copy).then_inc(s_hi, 1)
                        if j % NG == 0:
                            act.wait_ge(s_norm, b * 2 + j // NG + 1)
                        act.wait_ge(s_hi, b * NP + j + 1 + 4)
                        nc.scalar.activation(squares[:, j, :], qk_hi[:, j, :].bitcast(FP32), ACT.Square).then_inc(s_sq, 1)
                    else:
                        if j == 2 * NG:
                            act.wait_ge(s_vst, b * 16 + 16)
                        nc.scalar.activation(v_out[:, j - 2 * NG, :], prod_bank[j % 4], ACT.Copy).then_inc(s_hi, 1)
                    if j == NP - 2:
                        split_x(b + 1, 1 - par)
        act.wait_ge(s_top, 5)
        nc.scalar.activation(bound[:], bound_sq[:], ACT.Sqrt).then_inc(s_bound, 1)

    @block.vector
    def _(dve):
        dve.sem_inc(s_xlo, 2)
        dve.sem_inc(s_max, 2)
        dve.sem_inc(s_norm, 2)
        dve.sem_inc(s_qst, 32)
        dve.sem_inc(s_kst, 32)
        dve.sem_inc(s_vst, 16)
        dve.wait_ge(s_w[3], 16)
        nc.vector.tensor_scalar(w_in[:, 3], w_in[:, 3], 0.0, 2.0, ALU.is_ge, ALU.mult).then_inc(s_sign, 1)
        for u in range(4 * DC):
            m, c = divmod(u, DC)
            if m < 3:
                dve.wait_ge(s_whi, u + 1)
                nc.vector.tensor_tensor(w_lo[:, m, c, :], banks[:, u % 2, :], w_hi[:, m, c, :].bitcast(FP32),
                                        ALU.subtract).then_inc(s_wdone, 1)
            else:
                dve.wait_ge(s_wT, u + 1)
                if c == 0:
                    dve.wait_ge(s_ffn, 48)
                nc.vector.scalar_tensor_tensor(out=wf_scaled[:, c % 2, :], in0=banks[:, u % 2, :], scalar=-1.0, in1=scale_b[:],
                                               op0=ALU.add, op1=ALU.mult).then_inc(s_scaled, 1)
                dve.wait_ge(s_scaled, 2 * c + 1)
                nc.vector.tensor_copy(wf_hi[:, c, :], wf_scaled[:, c % 2, :]).then_inc(s_scaled, 1)
                dve.wait_ge(s_scaled, 2 * c + 2)
                nc.vector.tensor_tensor(wf_lo[:, c, :], wf_scaled[:, c % 2, :], wf_hi[:, c, :].bitcast(FP32),
                                        ALU.subtract).then_inc(s_wdone, 1)
        dve.wait_ge(s_hsum, G + 3)
        nc.vector.tensor_copy(bias_rows[0:1, :], bias_in[0:1, :]).then_inc(s_bias, 1)
        nc.vector.tensor_copy(bias_rows[HD:HD + 1, :], bias_in[HD:HD + 1, :]).then_inc(s_bias, 1)
        dve.wait_ge(s_bias, 2)
        nc.vector.tensor_tensor(bias_rows[HD:HD + 1, :], bias_in[HD:HD + 1, :], bias_rows[HD:HD + 1, :].bitcast(FP32),
                                ALU.subtract).then_inc(s_bias, 1)
        def split_x(b, par):
            for c in range(DC):
                dve.wait_ge(s_xhi, b * DC + c + 1)
                nc.vector.tensor_tensor(xT_lo[:, par, c, :], banks[:, c % 2, :], xT_hi[:, par, c, :].bitcast(FP32),
                                        ALU.subtract).then_inc(s_xlo, 1)

        def largest(b, half):
            dve.wait_ge(s_norm, b * 2 + half + 1 + 2)
            nc.vector.reduce_max(norms[:, half, bass.ds(b, 1)], banks[:, 6 + half, :], AX.X).then_inc(s_max, 1)

        split_x(0, 0)
        with dve.Fori(0, NBLK // 2) as pair:
            for par in range(2):
                b = pair * 2 + par
                for j in range(2 * NG):
                    dve.wait_ge(s_hi, b * NP + j + 1 + 4)
                    nc.vector.tensor_tensor(qk_lo[:, j, :], prod_bank[j % 4], qk_hi[:, j, :].bitcast(FP32),
                                            ALU.subtract).then_inc(s_lo, 1)
                largest(b, 0)
                largest(b, 1)
                split_x(b + 1, 1 - par)
        dve.wait_ge(s_max, 2 * NBLK + 2)
        nc.vector.reduce_max(top[:], norms[:], AX.X).then_inc(s_top, 1)
        dve.wait_ge(s_topT, 1)
        nc.vector.reduce_max(top_both[:], banks[0:1, 0, 0:2 * P].rearrange("o (i p) -> o i p", i=2), AX.X).then_inc(s_top, 1)
        dve.wait_ge(s_top, 2)
        nc.vector.tensor_tensor(top_product[:], top_both[:, 0:1], top_both[:, 1:2], ALU.mult).then_inc(s_top, 1)
        dve.wait_ge(s_topT, 2)
        nc.vector.tensor_scalar(flag[:], banks[0:1, 1, 0:1], BOUND_SLACK, BOUND_SQ_MAX, ALU.mult, ALU.is_gt).then_inc(s_top, 1)
        nc.vector.tensor_scalar(bound_sq[:], banks[:, 1, 0:1], BOUND_SLACK, BOUND_SQ_MAX, ALU.mult, ALU.min).then_inc(s_top, 1)
        dve.wait_ge(s_bound, 1)
        nc.vector.tensor_scalar(bound[:], bound[:], -SHIFT, None, ALU.mult).then_inc(s_top, 1)
        dve.wait_ge(s_top, 6)
        dve.wait_ge(s_const, 5)
        nc.vector.tensor_scalar(shift_rows[:], zero_rows[:], bound[0:N * H, :], None, ALU.add).then_inc(s_top, 1)


def exact_maxima(nc, ctx, dram, banks):

    def sb(name, shape, dt):
        return ctx.enter_context(nc.sbuf_tensor(name, shape, dt))

    def sem(name):
        return ctx.enter_context(nc.semaphore(name))

    q_head = sb("q_head", [3 * HD, S], FP32R)
    k_head = sb("k_head", [3 * HD, S], FP32R)
    maxima = sb("maxima", [P, KT], FP32)
    max_hi = sb("max_hi", [KT, P], FP32R)
    max_lo = sb("max_lo", [KT, P], FP32R)
    ident2 = sb("ident2", [P, P], FP32)
    flag = dram["flag"]

    m_id = sem("m_id")
    m_load = sem("m_load")
    m_score = sem("m_score")
    m_max = sem("m_max")
    m_T = sem("m_T")
    m_hi = sem("m_hi")
    m_lo = sem("m_lo")
    m_store = sem("m_store")

    block = ctx.enter_context(nc.Block())

    @block.sync
    def _(sp):
        needed = sp.value_load(flag[0:1, 0:1])
        with sp.If(needed > 0):
            with sp.Fori(0, N * H) as h:
                sp.wait_ge(m_store, h * 32 + 32)
                for r, (qs, ks) in enumerate((("q_hi", "k_hi"), ("q_lo", "k_hi"), ("q_hi", "k_lo"))):
                    for dst, src in ((q_head, qs), (k_head, ks)):
                        rows = dram[src].rearrange("n (h r) t -> (n h) r t", r=HD)[bass.ds(h, 1)]
                        sp.dma_start(dst[HD * r:HD * r + HD, :].bitcast(FP32), rows.rearrange("o r t -> (o r) t")).then_inc(m_load, 16)
                sp.wait_ge(m_lo, h + 2)
                for part, src in ((0, max_hi), (1, max_lo)):
                    row = dram["shift"][part][bass.ds(h, 1)].rearrange("o (t p) -> (o t) p", p=P)
                    sp.dma_start(row, src[:].bitcast(FP32)).then_inc(m_store, 16)
            sp.wait_ge(m_store, 32 * N * H + 32)

    @block.gpsimd
    def _(pool):
        nc.gpsimd.memset(ident2[:], 0.0).then_inc(m_id, 1)
        pool.wait_ge(m_id, 1)
        nc.gpsimd.affine_select(out=ident2[:], in_=ident2[:], compare_op=ALU.not_equal, fill=1.0, base=0,
                                pattern=[[-1, P]], channel_multiplier=1).then_inc(m_id, 1)
        pool.sem_inc(m_store, 32)
        pool.sem_inc(m_max, 2)
        pool.sem_inc(m_lo, 1)

    @block.tensor
    def _(pe):
        needed = pe.value_load(flag[0:1, 0:1])
        with pe.If(needed > 0):
            pe.wait_ge(m_id, 2)
            with pe.Fori(0, N * H) as h:
                pe.wait_ge(m_load, h * 96 + 96)
                for t in range(KT):
                    pe.wait_ge(m_max, h * KT + t + 1)
                    if t == 0:
                        pe.wait_ge(m_lo, h + 1)
                    for kb in range(QB):
                        last = nc.tensor.matmul(banks[:, 4 * (t % 2) + kb, :], q_head[:, t * P:(t + 1) * P],
                                                k_head[:, kb * BLK:(kb + 1) * BLK], start=True, stop=True)
                    last.then_inc(m_score, 1)
                pe.wait_ge(m_max, h * KT + KT + 2)
                nc.tensor.transpose(banks[0:KT, 0, 0:P], maxima[:], ident2[:]).then_inc(m_T, 1)

    @block.vector
    def _(dve):
        needed = dve.value_load(flag[0:1, 0:1])
        with dve.If(needed > 0):
            with dve.Fori(0, N * H) as h:
                for t in range(KT):
                    dve.wait_ge(m_score, h * KT + t + 1)
                    nc.vector.reduce_max(maxima[:, t:t + 1], banks[:, 4 * (t % 2):4 * (t % 2) + 4, :]
                                         .rearrange("p b k -> p (b k)"), AX.X).then_inc(m_max, 1)
                dve.wait_ge(m_T, h + 1)
                dve.wait_ge(m_store, h * 32 + 32)
                nc.vector.tensor_scalar(max_hi[:], banks[0:KT, 0, 0:P], -1.0, None, ALU.mult).then_inc(m_hi, 1)
                dve.wait_ge(m_hi, h + 1)
                nc.vector.scalar_tensor_tensor(out=max_lo[:], in0=banks[0:KT, 0, 0:P], scalar=-1.0, in1=max_hi[:].bitcast(FP32),
                                               op0=ALU.mult, op1=ALU.subtract).then_inc(m_lo, 1)


def attend(nc, ctx, dram, banks):

    def sb(name, shape, dt):
        return ctx.enter_context(nc.sbuf_tensor(name, shape, dt))

    def sem(name):
        return ctx.enter_context(nc.semaphore(name))

    q_rows = sb("q_rows", [KROWS, G, S], FP32R)
    k_rows = sb("k_rows", [KROWS, G, S], FP32R)
    v_keys = sb("v_keys", [P, KT, P], FP32)
    probs = sb("probs", [P, P_RING, G, BLK], FP32)
    sums = sb("sums", [P, 2, G, BLK], FP32)
    ones = sb("ones", [P, HD], FP32)
    out_sb = sb("out_sb", [P, 2, BLK], FP32)
    den_sb = sb("den_sb", [P, 2, BLK], FP32)

    a_one = sem("a_one")
    a_q = [sem(f"a_q{c}") for c in range(QB)]
    a_k = [sem(f"a_k{c}") for c in range(QB)]
    a_score = sem("a_score")
    a_prob = sem("a_prob")
    a_pv = sem("a_pv")
    a_sum = [sem(f"a_sum{h}") for h in range(2)]
    a_acc = sem("a_acc")
    a_den = sem("a_den")
    a_out = sem("a_out")
    a_dout = sem("a_dout")
    a_store = [sem(f"a_store{h}") for h in range(2)]

    UNITS = 2 * KT
    NV = KT - PE_DEN
    STEP_Q = 4 * 16
    STEP_K = 4 * 16

    def scores_of(u):
        return banks[:, 2 * (u % SLOTS):2 * (u % SLOTS) + 2, :]

    OUT_BANK, DEN_BANK = 2 * SLOTS, 2 * SLOTS + 1

    block = ctx.enter_context(nc.Block())

    @block.sync
    def _(sp):
        v_src = dram["v"].rearrange("(n b) (t p) (g d) -> n g b p t d", n=N, p=P, g=NG)

        def load_q(it, c):
            cols = slice(c * BLK, (c + 1) * BLK)
            for r, part in enumerate(("q_hi", "q_lo", "q_hi")):
                src = dram[part].rearrange("n (g h r) t -> (n g) r h t", g=NG, r=HD)[bass.ds(it, 1), :, :, cols]
                sp.dma_start(q_rows[HD * r:HD * r + HD, :, cols].bitcast(FP32), src.rearrange("o r h t -> (o r) h t")).then_inc(a_q[c], 16)
            src = dram["shift"].rearrange("s (i h) t -> i s h t", h=G)[bass.ds(it, 1), :, :, cols]
            sp.dma_start(q_rows[3 * HD:KROWS, :, cols].bitcast(FP32), src.rearrange("o s h t -> (o s) h t")).then_inc(a_q[c], 16)

        def load_k(it, c):
            cols = slice(c * BLK, (c + 1) * BLK)
            for r, part in enumerate(("k_hi", "k_hi", "k_lo")):
                src = dram[part].rearrange("n (g h r) t -> (n g) r h t", g=NG, r=HD)[bass.ds(it, 1), :, :, cols]
                sp.dma_start(k_rows[HD * r:HD * r + HD, :, cols].bitcast(FP32), src.rearrange("o r h t -> (o r) h t")).then_inc(a_k[c], 16)

        def load_v(n, g, c):
            src = v_src[bass.ds(n, 1), bass.ds(g, 1), c].rearrange("o u p t d -> p (o u t) d")
            sp.dma_start(v_keys[:, c * TPB:(c + 1) * TPB, :], src).then_inc(a_k[c], 16)

        def store(it, qb):
            cols = slice(qb * BLK, (qb + 1) * BLK)
            sp.wait_ge(a_out, it * QB + qb + 1 + 1)
            dst = dram["attn"].rearrange("n (g p) t -> (n g) p t", p=P)[bass.ds(it, 1), :, cols]
            sp.dma_start(dst.rearrange("o p t -> (o p) t"), out_sb[:, qb % 2, :]).then_inc(a_store[qb % 2], 16)
            sp.wait_ge(a_dout, it * QB + qb + 1 + 1)
            dst = dram["den"].rearrange("(i h) t -> i h t", h=G)[bass.ds(it, 1), :, cols]
            sp.dma_start(dst.rearrange("o h t -> (o h) t"), den_sb[0:P:HD, qb % 2, :]).then_inc(a_store[qb % 2], 16)

        for c in range(QB):
            load_q(0, c)
            load_k(0, c)
            load_v(0, 0, c)
        with sp.Fori(0, ITEMS - 1) as it:
            ahead = sp.snap(it + 1)
            n_ahead = sp.snap((it + 1) // NG)
            g_ahead = sp.snap((it + 1) % NG)
            for qb in range(QB):
                st = it * QB + qb
                if qb == QB - 1:
                    for c in range(QB):
                        sp.wait_ge(a_score, st * UNITS + 2 * TPB * (c + 1))
                        load_k(ahead, c)
                        if c > 0:
                            sp.wait_ge(a_pv, st * KT + TPB * c + P_RING)
                            load_v(n_ahead, g_ahead, c - 1)
                sp.wait_ge(a_score, st * UNITS + UNITS)
                load_q(ahead, qb)
                if qb < QB - 1:
                    store(it, qb)
            sp.wait_ge(a_pv, (it * QB + QB) * KT + P_RING)
            load_v(n_ahead, g_ahead, QB - 1)
            store(it, QB - 1)
        for qb in range(QB):
            store(ITEMS - 1, qb)
        for h in range(2):
            sp.wait_ge(a_store[h], ITEMS * QB // 2 * 32 + 32)

    @block.gpsimd
    def _(pool):
        nc.gpsimd.memset(ones[:], 1.0).then_inc(a_one, 1)
        pool.wait_ge(a_one, 1)
        nc.gpsimd.memset(k_rows[3 * HD:KROWS, :, :].bitcast(FP32), 1.0).then_inc(a_one, 1)

    @block.tensor
    def _(pe):
        pe.sem_inc(a_pv, P_RING)
        pe.sem_inc(a_den, 2)
        pe.wait_ge(a_one, 2)

        def scores(it, qb, kt):
            st = it * QB + qb
            if kt == 0:
                pe.wait_ge(a_q[qb], it * STEP_Q + STEP_Q)
            if qb == 0 and kt % TPB == 0:
                pe.wait_ge(a_k[kt // TPB], it * STEP_K + STEP_K)
            for u in (2 * kt, 2 * kt + 1):
                before = u - SLOTS if u >= SLOTS else max(v for v in range(UNITS) if v % SLOTS == u) - UNITS
                pe.wait_ge(a_prob, st * UNITS + before + 1 + SLOTS)
                for i in range(2):
                    h = u % 2 * 2 + i
                    last = nc.tensor.matmul(scores_of(u)[:, i, :], k_rows[:, h, kt * P:(kt + 1) * P],
                                            q_rows[:, h, qb * BLK:(qb + 1) * BLK], start=True, stop=True)
                last.then_inc(a_score, 1)

        def values(it, qb, kt):
            st = it * QB + qb
            pe.wait_ge(a_prob, st * UNITS + 2 * kt + 2 + SLOTS)
            if kt == 0:
                pe.wait_ge(a_out, st + 1)
            for h in range(G):
                rows = slice(HD * h, HD * h + HD)
                last = nc.tensor.matmul(banks[rows, OUT_BANK, :], v_keys[:, kt, rows], probs[:, kt % P_RING, h, :],
                                        start=(kt == 0), stop=(kt == KT - 1))
            if kt == KT - 1:
                last.then_inc(a_acc, 1)
            if kt >= NV:
                if kt == NV:
                    pe.wait_ge(a_dout, st + 1)
                for h in range(G):
                    rows = slice(HD * h, HD * h + HD)
                    last = nc.tensor.matmul(banks[rows, DEN_BANK, :], ones[:], probs[:, kt % P_RING, h, :],
                                            start=(kt == NV), stop=False)
            last.then_inc(a_pv, 1)

        def denominators(it, qb):
            st = it * QB + qb
            for half in range(2):
                pe.wait_ge(a_sum[half], (st + 1) * NV + P_RING)
            for h in range(G):
                rows = slice(HD * h, HD * h + HD)
                last = nc.tensor.matmul(banks[rows, DEN_BANK, :], ones[:], sums[:, qb % 2, h, :], start=False, stop=True)
            last.then_inc(a_den, 1)

        def steps(it, qb, tiles):
            for kt in tiles:
                if kt + LAG < KT:
                    scores(it, qb, kt + LAG)
                elif qb < QB - 1:
                    scores(it, qb + 1, kt + LAG - KT)
                elif it is not LAST:
                    scores(it + 1, 0, kt + LAG - KT)
                values(it, qb, kt)

        def item(it):
            for qb in range(QB):
                if qb > 0:
                    steps(it, qb, range(DEN_LAG))
                    denominators(it, qb - 1)
                steps(it, qb, range(DEN_LAG, KT))
            if it is not LAST:
                steps(it + 1, 0, range(DEN_LAG))
            denominators(it, QB - 1)

        LAST = ITEMS - 1
        for kt in range(LAG):
            scores(0, 0, kt)
        steps(0, 0, range(DEN_LAG))
        with pe.Fori(0, ITEMS - 1) as it:
            item(it)
        item(LAST)

    @block.scalar
    def _(act):
        act.sem_inc(a_prob, SLOTS)
        act.sem_inc(a_out, 1)
        act.sem_inc(a_dout, 1)

        def copy_out(st, parity):
            act.wait_ge(a_acc, st + 1)
            act.wait_ge(a_store[parity], (st - parity) * 16 + 32)
            nc.scalar.activation(out_sb[:, parity, :], banks[:, OUT_BANK, :], ACT.Copy).then_inc(a_out, 1)

        def copy_den(st, parity):
            act.wait_ge(a_den, st + 1 + 2)
            act.wait_ge(a_store[parity], (st - parity) * 16 + 32)
            nc.scalar.activation(den_sb[:, parity, :], banks[:, DEN_BANK, :], ACT.Copy).then_inc(a_dout, 1)

        def item(it, first):
            for qb in range(QB):
                st = it * QB + qb
                for u in range(UNITS):
                    kt, half = divmod(u, 2)
                    act.wait_ge(a_score, st * UNITS + u + 1)
                    before = kt - P_RING if kt >= P_RING else max(v for v in range(KT) if v % P_RING == kt) - KT
                    if half == 0:
                        act.wait_ge(a_pv, st * KT + before + 1 + P_RING)
                    summed = min(before + 1, NV) if before >= 0 else min(before + KT + 1, NV) - NV
                    act.wait_ge(a_sum[half], st * NV + summed + P_RING)
                    heads = slice(2 * half, 2 * half + 2)
                    nc.scalar.activation(probs[:, kt % P_RING, heads, :], scores_of(u), ACT.Exp, scale=SCALE).then_inc(a_prob, 1)
                    if u == 2 * LAG - 1 and not (first and qb == 0):
                        copy_out(st - 1, (qb - 1) % 2)
                    if u == 2 * (LAG + DEN_LAG) + 1 and not (first and qb == 0):
                        copy_den(st - 1, (qb - 1) % 2)

        item(0, True)
        with act.Fori(1, ITEMS) as it:
            item(it, False)
        copy_out(ITEMS * QB - 1, 1)
        copy_den(ITEMS * QB - 1, 1)

    @block.vector
    def _(dve):
        dve.sem_inc(a_sum[0], P_RING)
        dve.sem_inc(a_sum[1], P_RING)
        dve.sem_inc(a_store[0], 32)
        dve.sem_inc(a_store[1], 32)

        with dve.Fori(0, ITEMS) as it:
            for qb in range(QB):
                st = it * QB + qb
                for kt in range(1, NV):
                    for half in range(2):
                        heads = slice(2 * half, 2 * half + 2)
                        total = sums[:, qb % 2, heads, :]
                        dve.wait_ge(a_prob, st * UNITS + 2 * kt + half + 1 + SLOTS)
                        if kt == 1:
                            dve.wait_ge(a_den, st + 1)
                            nc.vector.tensor_tensor(total, probs[:, 0, heads, :], probs[:, 1, heads, :], ALU.add).then_inc(a_sum[half], 2)
                        else:
                            dve.wait_ge(a_sum[half], st * NV + kt + P_RING)
                            nc.vector.tensor_tensor(total, total, probs[:, kt % P_RING, heads, :], ALU.add).then_inc(a_sum[half], 1)


def normalise_and_ffn(nc, ctx, dram, x, ffn, banks, out):
    wf_hi, wf_lo, bias_ones, bias_rows = ffn

    def sb(name, shape, dt):
        return ctx.enter_context(nc.sbuf_tensor(name, shape, dt))

    def sem(name):
        return ctx.enter_context(nc.semaphore(name))

    T = 2 * QB * TPB
    ROUNDS = N * S // P // T
    RB = T // TPB
    Y_SLOTS = 8
    ident3 = sb("ident3", [P, P], FP32)
    eps = sb("eps", [P, 1], FP32)
    x_in = sb("x_res", [P, 2, TPB, D], FP32)
    attnT = sb("attnT", [P, 2, DC, BLK], FP32)
    den_in = sb("den_in", [H, 2, BLK], FP32)
    rden = sb("rden", [P, 2, H], FP32)
    attn = sb("attn", [P, 2, D], FP32)
    res1 = sb("res1", [P, 2, D], FP32)
    y = sb("y", [P, Y_SLOTS, D], FP32)
    yT_hi = sb("yT_hi", [P, 4, D], FP32R)
    yT_lo = sb("yT_lo", [P, 4, D], FP32R)
    clipped = sb("clipped", [P, 2, D], FP32)
    res2 = sb("res2", [P, 2, D], FP32)
    y2 = sb("y2", [P, 4, D], FP32)
    stats = sb("stats", [P, 2, 2, 6], FP32)
    mean_var = sb("mean_var", [P, 2, 2, 2], FP32)
    std = sb("std", [P, 2, 2, 1], FP32)
    rstd = sb("rstd", [P, 2, 2, 1], FP32)
    offset = sb("offset", [P, 2, 2, 1], FP32)

    f_const = sem("f_const")
    f_in = [sem(f"f_in{k}") for k in range(2)]
    f_aT = sem("f_aT")
    f_rden = sem("f_rden")
    f_attn = sem("f_attn")
    f_res = [sem("f_res1"), sem("f_res2")]
    f_stat = [sem("f_stat1"), sem("f_stat2")]
    f_order = sem("f_order")
    f_std = [sem("f_std1"), sem("f_std2")]
    f_rstd = [sem("f_rstd1"), sem("f_rstd2")]
    f_y = [sem("f_y1"), sem("f_y2")]
    f_yT = sem("f_yT")
    f_yhi = sem("f_yhi")
    f_ylo = sem("f_ylo")
    f_ffn = sem("f_ffn")
    f_clip = sem("f_clip")
    f_out = [sem(f"f_out{k}") for k in range(4)]

    def aT_bank(t):
        return banks[:, t % 2, :]

    def den_bank(t):
        return banks[:, 6 + t % 2, 0:H]

    def yT_bank(t):
        return banks[:, 2 + t % 2, :]

    def ffn_bank(t):
        return banks[:, 4 + t % 2, :]

    ATTN, LN1, TRANS, FFN, CLIP, LN2 = 0, 1, 2, 4, 5, 6

    def tile_of(i, lag):
        return i - lag if 0 <= i - lag < T else None

    block = ctx.enter_context(nc.Block())

    @block.sync
    def _(sp):
        with sp.Fori(0, ROUNDS) as r:
            for j in range(RB):
                blk = sp.snap(r * RB + j)
                batch = sp.snap(r * (RB // QB) + j // QB)
                cols = slice(j % QB * BLK, (j % QB + 1) * BLK)
                k = j % 2
                sp.wait_ge(f_res[0], r * T + j * TPB + TPB)
                src = dram["attn"][bass.ds(batch, 1), :, cols].rearrange("o (c p) t -> p (o c) t", p=P)
                sp.dma_start(attnT[:, k], src).then_inc(f_in[k], 16)
                src = dram["den"].rearrange("(n h) t -> n h t", n=N)[bass.ds(batch, 1), :, cols]
                sp.dma_start(den_in[:, k], src.rearrange("o h t -> (o h) t")).then_inc(f_in[k], 16)
                sp.dma_start(x_in[:, k], x[bass.ds(blk, 1)].rearrange("o p t d -> p (o t) d")).then_inc(f_in[k], 16)

    @block.gpsimd
    def _(pool):
        nc.gpsimd.memset(ident3[:], 0.0).then_inc(f_const, 1)
        nc.gpsimd.memset(eps[:], EPS).then_inc(f_const, 1)
        pool.sem_inc(f_res[0], 2 * TPB)
        pool.sem_inc(f_res[1], Y_SLOTS)
        pool.wait_ge(f_const, 2)
        nc.gpsimd.affine_select(out=ident3[:], in_=ident3[:], compare_op=ALU.not_equal, fill=1.0, base=0,
                                pattern=[[-1, P]], channel_multiplier=1).then_inc(f_const, 1)
        with pool.Fori(0, ROUNDS) as r:
            for i in range(T + LN2):
                if (t := tile_of(i, CLIP)) is not None:
                    pool.wait_ge(f_clip, r * T + t + 1 + 2)
                    pool.wait_ge(f_y[1], r * T + t + 1)
                    nc.gpsimd.tensor_tensor(res2[:, t % 2], clipped[:, t % 2], y[:, t % Y_SLOTS], ALU.add).then_inc(f_res[1], 1)
                if (t := tile_of(i, ATTN)) is not None:
                    pool.wait_ge(f_attn, r * T + t + 1 + 2)
                    pool.wait_ge(f_y[0], r * T + t + 1)
                    nc.gpsimd.tensor_tensor(res1[:, t % 2], attn[:, t % 2], x_in[:, t // TPB % 2, t % TPB], ALU.add).then_inc(f_res[0], 1)

    @block.tensor
    def _(pe):
        pe.sem_inc(f_ffn, 4)
        pe.wait_ge(f_const, 3)
        with pe.Fori(0, ROUNDS) as r:
            for i in range(T + LN2):
                if (t := tile_of(i, ATTN)) is not None:
                    k = t // TPB % 2
                    cols = slice(t % TPB * P, (t % TPB + 1) * P)
                    if t % TPB == 0:
                        pe.wait_ge(f_in[k], r * (RB // 2 * 48) + t // TPB // 2 * 48 + 48)
                    pe.wait_ge(f_attn, r * T + t + 1)
                    for c in range(DC):
                        nc.tensor.transpose(aT_bank(t)[:, c * P:(c + 1) * P], attnT[:, k, c, cols], ident3[:])
                    nc.tensor.transpose(den_bank(t), den_in[:, k, cols], ident3[0:H, 0:H]).then_inc(f_aT, 1)
                if (t := tile_of(i, TRANS)) is not None:
                    pe.wait_ge(f_y[0], r * T + t + 1 + 2)
                    pe.wait_ge(f_ylo, r * T + t + 1)
                    for c in range(DC):
                        last = nc.tensor.transpose(yT_bank(t)[:, c * P:(c + 1) * P], y[:, t % Y_SLOTS, c * P:(c + 1) * P], ident3[:])
                    last.then_inc(f_yT, 1)
                if (t := tile_of(i, FFN)) is not None:
                    pe.wait_ge(f_ylo, r * T + t + 1 + 2)
                    pe.wait_ge(f_clip, r * T + t + 1)
                    nc.tensor.matmul(ffn_bank(t), bias_ones[:], bias_rows[:], start=True, stop=False)
                    for c in range(DC):
                        cols = slice(c * P, (c + 1) * P)
                        for part, w in ((yT_hi, wf_hi), (yT_lo, wf_hi), (yT_hi, wf_lo)):
                            last = nc.tensor.matmul(ffn_bank(t), part[:, t % 4, cols], w[:, c, :], start=False,
                                                    stop=(c == DC - 1 and w is wf_lo))
                    last.then_inc(f_ffn, 1)

    @block.scalar
    def _(act):
        act.sem_inc(f_y[0], 2)
        act.sem_inc(f_y[1], 2)

        def deviation(r, t, which):
            act.wait_ge(f_stat[which], (r * T + t + 1) * 2)
            act.wait_ge(f_rstd[which], (r * T + t + 1) * 2)
            nc.scalar.activation(std[:, t % 2, which], mean_var[:, t % 2, which, 1:2], ACT.Sqrt, bias=eps[:]).then_inc(f_std[which], 1)

        def layernorm(r, t, which, src, dst, slots):
            act.wait_ge(f_rstd[which], (r * T + t + 1) * 2 + 4)
            nc.scalar.activation(dst[:, t % slots], src[:, t % 2], ACT.Identity, scale=rstd[:, t % 2, which],
                                 bias=offset[:, t % 2, which]).then_inc(f_y[which], 1)

        act.wait_ge(f_const, 2)
        with act.Fori(0, ROUNDS) as r:
            for i in range(T + LN2):
                if (t := tile_of(i, LN1)) is not None:
                    deviation(r, t, 0)
                if (t := tile_of(i, LN2)) is not None:
                    deviation(r, t, 1)
                if (t := tile_of(i, TRANS)) is not None:
                    act.wait_ge(f_yT, r * T + t + 1)
                    act.wait_ge(f_ffn, r * T + t + 1)
                    nc.scalar.activation(yT_hi[:, t % 4], yT_bank(t), ACT.Copy).then_inc(f_yhi, 1)
                if (t := tile_of(i, LN1)) is not None:
                    act.wait_ge(f_res[1], r * T + t + 1)
                    layernorm(r, t, 0, res1, y, Y_SLOTS)
                if (t := tile_of(i, LN2)) is not None:
                    act.wait_ge(f_out[t % 4], r * (T // 4 * 16) + t // 4 * 16 + 16)
                    layernorm(r, t, 1, res2, y2, 4)
                    row = act.snap(r * T + t)
                    act.wait_ge(f_y[1], r * T + t + 1 + 2)
                    act.dma_start(out[bass.ds(row, 1)].rearrange("o p d -> (o p) d"), y2[:, t % 4]).then_inc(f_out[t % 4], 16)
        for k in range(4):
            act.wait_ge(f_out[k], ROUNDS * T // 4 * 16 + 16)

    @block.vector
    def _(dve):
        dve.sem_inc(f_attn, 2)
        dve.sem_inc(f_ylo, 2)
        dve.sem_inc(f_clip, 2)
        for which in range(2):
            dve.sem_inc(f_rstd[which], 4)
        for k in range(4):
            dve.sem_inc(f_out[k], 16)

        def statistics(r, t, which, src, credit):
            dve.wait_ge(f_res[which], r * T + t + 1 + credit)
            nc.vector.bn_stats(stats[:, t % 2, which], src[:, t % 2]).then_inc(f_stat[which], 1)

        def aggregate(r, t, which):
            dve.wait_ge(f_stat[which], (r * T + t) * 2 + 1)
            dve.sem_inc(f_order, 1)
            nc.vector.bn_aggr(mean_var[:, t % 2, which], stats[:, t % 2, which]).then_inc(f_stat[which], 1)

        def reciprocal_std(r, t, which):
            dve.wait_ge(f_std[which], r * T + t + 1)
            dve.wait_ge(f_y[which], r * T + t + 1)
            nc.vector.reciprocal(rstd[:, t % 2, which], std[:, t % 2, which]).then_inc(f_rstd[which], 1)

        def offset_of(r, t, which):
            dve.wait_ge(f_rstd[which], (r * T + t) * 2 + 1 + 4)
            nc.vector.scalar_tensor_tensor(out=offset[:, t % 2, which], in0=mean_var[:, t % 2, which, 0:1], scalar=-1.0,
                                           in1=rstd[:, t % 2, which], op0=ALU.mult, op1=ALU.mult).then_inc(f_rstd[which], 1)

        with dve.Fori(0, ROUNDS) as r:
            for i in range(T + LN2):
                attn_t, ln1_t, trans_t, clip_t, ln2_t = (tile_of(i, lag) for lag in (ATTN, LN1, TRANS, CLIP, LN2))
                norms = [(t, which) for t, which in ((ln1_t, 0), (ln2_t, 1)) if t is not None]
                if (t := clip_t) is not None:
                    dve.wait_ge(f_ffn, r * T + t + 1 + 4)
                    dve.wait_ge(f_res[1], r * T + t + 1 - 2 + Y_SLOTS)
                    nc.vector.tensor_scalar(clipped[:, t % 2], ffn_bank(t), -MAX_VAL, MAX_VAL, ALU.max, ALU.min).then_inc(f_clip, 1)
                for t, which in norms:
                    statistics(r, t, which, (res1, res2)[which], (2 * TPB, Y_SLOTS)[which])
                if (t := attn_t) is not None:
                    dve.wait_ge(f_aT, r * T + t + 1)
                    dve.wait_ge(f_attn, r * T + t + 1)
                    nc.vector.reciprocal(rden[:, t % 2], den_bank(t)).then_inc(f_rden, 1)
                for t, which in norms:
                    aggregate(r, t, which)
                if (t := attn_t) is not None:
                    dve.wait_ge(f_rden, r * T + t + 1)
                    dve.wait_ge(f_res[0], r * T + t + 1 - 2 + 2 * TPB)
                    nc.vector.tensor_tensor(attn[:, t % 2].rearrange("p (h d) -> p h d", h=H),
                                            aT_bank(t).rearrange("p (h d) -> p h d", h=H),
                                            rden[:, t % 2].unsqueeze(2).to_broadcast([P, H, HD]), ALU.mult).then_inc(f_attn, 1)
                for t, which in norms:
                    reciprocal_std(r, t, which)
                for t, which in norms:
                    offset_of(r, t, which)
                if (t := trans_t) is not None:
                    dve.wait_ge(f_yhi, r * T + t + 1)
                    nc.vector.tensor_tensor(yT_lo[:, t % 4], yT_bank(t), yT_hi[:, t % 4].bitcast(FP32), ALU.subtract).then_inc(f_ylo, 1)


def build(nc, x, Wq, Wk, Wv, Wf, scale, bias, out):
    def scratch(name, shape, dt):
        return nc.dram_tensor("scratch_" + name, shape, dt, kind="Internal").ap()

    x_blocks = x.rearrange("n (b t p) d -> (n b) p t d", p=P, t=TPB)
    out_tiles = out.rearrange("n (t p) d -> (n t) p d", p=P)
    dram = {k: scratch(k, (N, D, S), FP32) for k in ("q_hi", "q_lo", "k_hi", "k_lo")}
    dram["v"] = scratch("v", (NBLK, BLK, D), FP32)
    dram["shift"] = scratch("shift", (2, N * H, S), FP32)
    dram["attn"] = scratch("attn", (N, D, S), FP32)
    dram["den"] = scratch("den", (N * H, S), FP32)
    with ExitStack() as whole:
        banks = whole.enter_context(nc.psum_tensor("banks", [P, 8, BLK], FP32))
        ffn = [whole.enter_context(nc.sbuf_tensor(name, shape, FP32R)) for name, shape in (
            ("wf_hi", [P, DC, D]), ("wf_lo", [P, DC, D]), ("bias_ones", [2 * HD, P]), ("bias_rows", [2 * HD, D]))]
        dram["flag"] = whole.enter_context(nc.sbuf_tensor("flag", [1, 1], INT32))
        with ExitStack() as ctx:
            project(nc, ctx, dram, (x_blocks, Wq, Wk, Wv, Wf, scale, bias), banks, ffn)
        with ExitStack() as ctx:
            exact_maxima(nc, ctx, dram, banks)
        with ExitStack() as ctx:
            attend(nc, ctx, dram, banks)
        with ExitStack() as ctx:
            normalise_and_ffn(nc, ctx, dram, x_blocks, ffn, banks, out_tiles)


_INS = ["L0_attn_x", "L0_attn_Wq", "L0_attn_Wk", "L0_attn_Wv", "L0_ffn_weights", "L0_ffn_scale", "L0_ffn_bias"]


def kernel(**inputs):
    import numpy as np
    import concourse.bacc as bacc
    from concourse.bass_utils import run_bass_kernel_spmd

    nc = bacc.Bacc("TRN2", target_bir_lowering=False, num_devices=1)
    arrays, args = {}, []
    for name in _INS:
        a = np.ascontiguousarray(inputs[name])
        arrays[f"in_{name}"] = a
        args.append(nc.dram_tensor(f"in_{name}", a.shape, mybir.dt.from_np(a.dtype), kind="ExternalInput").ap())
    out = nc.dram_tensor("out_x", (N, S, D), FP32, kind="ExternalOutput").ap()
    build(nc, *args, out)
    r = run_bass_kernel_spmd(nc, [arrays], core_ids=[0])
    return r.results[0]["out_x"]
```

```python
import concourse.bass as bass
from concourse import mybir
from contextlib import ExitStack

FP32 = mybir.dt.float32
FP32R = mybir.dt.float32r
BF16 = mybir.dt.bfloat16
INT32 = mybir.dt.int32
ALU = mybir.AluOpType
ACT = mybir.ActivationFunctionType
AX = mybir.AxisListType

P = 128
N, S, D = 4, 2048, 512
H, HD = 16, 32
G = P // HD
NG = H // G
DC = D // P
BLK = 512
TPB = BLK // P
NBLK = N * S // BLK
QB = S // BLK
KT = S // P
ITEMS = N * NG
SCALE = float(HD) ** -0.5
EPS = 1e-5
MAX_VAL = 100.0
KROWS = 3 * HD + 2
SHIFT = 0.25
BOUND_MAX = 64.0
BOUND_SQ_MAX = (BOUND_MAX / SCALE) ** 2
BOUND_SLACK = 1.04
CHAINS = 2
P_RING = 8
SLOTS = 3
LAG = 2
DEN_TILE = 10


def project(nc, ctx, dram, args, banks, ffn):
    x, Wq, Wk, Wv, Wf, scale, bias = args
    _, _, bias_ones, bias_rows, wf_scaled = ffn

    def sb(name, shape, dt):
        return ctx.enter_context(nc.sbuf_tensor(name, shape, dt))

    def sem(name):
        return ctx.enter_context(nc.semaphore(name))

    ident = sb("ident", [P, P], FP32)
    head_sum = sb("head_sum", [P, HD], BF16)
    w_in = sb("w_in", [P, 4, DC, D], FP32)
    w_hi = sb("w_hi", [P, 3, DC, D], FP32R)
    w_lo = sb("w_lo", [P, 3, DC, D], FP32R)
    x_in = sb("x_in", [P, TPB, D], FP32)
    xT_hi = sb("xT_hi", [P, 2, DC, BLK], FP32R)
    xT_lo = sb("xT_lo", [P, 2, DC, BLK], FP32R)
    qk_hi = sb("qk_hi", [P, 2 * NG, BLK], FP32R)
    qk_lo = sb("qk_lo", [P, 2 * NG, BLK], FP32R)
    v_out = sb("v_out", [P, TPB, D], FP32)
    squares = sb("squares", [P, 2 * NG, BLK], BF16)
    norms = sb("norms", [P, 2, NBLK], FP32)
    top = sb("top", [P, 2], FP32)
    top_both = sb("top_both", [1, 2], FP32)
    top_product = sb("top_product", [1, 1], FP32)
    ones_row = sb("ones_row", [1, P], FP32)
    bound_sq = sb("bound_sq", [P, 1], FP32)
    bound = sb("bound", [P, 1], FP32)
    flag = dram["flag"]
    scale_b = sb("scale_b", [P, D], FP32)
    bias_in = sb("bias_in", [2 * HD, D], FP32)
    shift_rows = sb("shift_rows", [N * H, BLK], FP32R)
    zero_rows = sb("zero_rows", [N * H, BLK], FP32)

    s_const = sem("s_const")
    s_hsum = sem("s_hsum")
    s_w = [sem(f"s_w{m}") for m in range(4)]
    s_sign = sem("s_sign")
    s_ffn = sem("s_ffn")
    s_bias = sem("s_bias")
    s_scaled = sem("s_scaled")
    s_wT = sem("s_wT")
    s_whi = sem("s_whi")
    s_wdone = sem("s_wdone")
    s_x = sem("s_x")
    s_xT = sem("s_xT")
    s_xhi = sem("s_xhi")
    s_xlo = sem("s_xlo")
    s_prod = sem("s_prod")
    s_hi = sem("s_hi")
    s_sq = sem("s_sq")
    s_lo = sem("s_lo")
    s_norm = sem("s_norm")
    s_max = sem("s_max")
    s_qst, s_kst, s_vst = sem("s_qst"), sem("s_kst"), sem("s_vst")
    s_top = sem("s_top")
    s_topT = sem("s_topT")
    s_bound = sem("s_bound")
    s_shift = sem("s_shift")

    NP = 2 * NG + TPB
    prod_bank = [banks[:, 2 + j, :] for j in range(4)]
    X_STEPS = {2 * NG: range(2), NP - 2: range(2, DC)}

    def w_bank(u):
        return prod_bank[u % 4]

    block = ctx.enter_context(nc.Block())

    @block.sync
    def _(sp):
        for m, w in enumerate((Wq, Wk, Wv)):
            sp.dma_start(w_in[:, m], w.rearrange("(t p) i -> p t i", p=P)).then_inc(s_w[m], 16)
        sp.dma_start(x_in[:], x[0]).then_inc(s_x, 16)
        sp.dma_start(w_in[:, 3], Wf.rearrange("(t p) i -> p t i", p=P)).then_inc(s_w[3], 16)
        sp.dma_start(scale_b[:], scale.partition_broadcast(P)).then_inc(s_ffn, 16)
        for row in (0, HD):
            sp.dma_start(bias_in[row:row + 1, :], bias.partition_broadcast(1)).then_inc(s_ffn, 16)
        sp.wait_ge(s_const, 4)
        sp.dma_start(dram["shift"][1].rearrange("h (c t) -> h c t", c=QB),
                     zero_rows[:].unsqueeze(1).to_broadcast([N * H, QB, BLK])).then_inc(s_shift, 16)
        with sp.Fori(0, NBLK) as b:
            batch = sp.snap(b // QB)
            column = sp.snap((b % QB) * BLK)
            ahead = sp.snap((b + 1) % NBLK)
            sp.wait_ge(s_xT, b * DC + DC)
            sp.dma_start(x_in[:], x[bass.ds(ahead, 1)].rearrange("o p t d -> p (o t) d")).then_inc(s_x, 16)
            for first, hi, lo, store in ((0, "q_hi", "q_lo", s_qst), (NG, "k_hi", "k_lo", s_kst)):
                for part, src in ((hi, qk_hi), (lo, qk_lo)):
                    if first == 0:
                        sp.wait_ge(s_lo, b * 2 * NG + NG)
                    else:
                        sp.wait_ge(s_lo, b * 2 * NG + 2 * NG)
                    sp.dma_start(dram[part][bass.ds(batch, 1), :, bass.ds(column, BLK)]
                                 .rearrange("o (g p) t -> p (o g) t", p=P),
                                 src[:, first:first + NG, :].bitcast(FP32)).then_inc(store, 16)
            sp.wait_ge(s_hi, b * NP + NP + 4)
            sp.dma_start(dram["v"][bass.ds(b, 1)].rearrange("o (t p) d -> p (o t) d", p=P),
                         v_out[:]).then_inc(s_vst, 16)
        sp.wait_ge(s_qst, 32 * NBLK)
        sp.wait_ge(s_kst, 32 * NBLK)
        sp.wait_ge(s_vst, 16 * NBLK)
        sp.wait_ge(s_x, 16 * (NBLK + 1))
        sp.wait_ge(s_top, 7)
        sp.dma_start(dram["shift"][0].rearrange("h (c t) -> h c t", c=QB),
                     shift_rows[:].bitcast(FP32).unsqueeze(1).to_broadcast([N * H, QB, BLK])).then_inc(s_shift, 16)
        sp.wait_ge(s_shift, 32)

    @block.gpsimd
    def _(pool):
        nc.gpsimd.memset(ident[:], 0.0).then_inc(s_const, 1)
        nc.gpsimd.memset(head_sum[:], 0.0).then_inc(s_const, 1)
        nc.gpsimd.memset(ones_row[:], 1.0).then_inc(s_const, 1)
        nc.gpsimd.memset(zero_rows[:], 0.0).then_inc(s_const, 1)
        pool.wait_ge(s_const, 4)
        nc.gpsimd.affine_select(out=ident[:], in_=ident[:], compare_op=ALU.not_equal, fill=1.0, base=0,
                                pattern=[[-1, P]], channel_multiplier=1).then_inc(s_const, 1)
        for h in range(G):
            pool.wait_ge(s_const, 5)
            if h > 0:
                pool.wait_ge(s_hsum, h)
            cols = head_sum[HD * h:HD * h + HD, :].rearrange("p (r h) -> p h r", h=G)[:, h, :]
            nc.gpsimd.memset(cols, 1.0).then_inc(s_hsum, 1)
        pool.wait_ge(s_hsum, G)
        nc.gpsimd.memset(bias_ones[:].bitcast(FP32), 1.0).then_inc(s_hsum, 1)
        pool.wait_ge(s_hsum, G + 1)
        nc.gpsimd.memset(bias_rows[:].bitcast(FP32), 0.0).then_inc(s_hsum, 2)

    @block.tensor
    def _(pe):
        def transpose_w(u):
            m, c = divmod(u, DC)
            for t in range(DC):
                last = nc.tensor.transpose(w_bank(u)[:, t * P:(t + 1) * P], w_in[:, m, t, c * P:(c + 1) * P], ident[:])
            last.then_inc(s_wT, 1)

        pe.wait_ge(s_const, 5)
        for u in range(3 * DC):
            if u % DC == 0:
                pe.wait_ge(s_w[u // DC], 16)
            if u >= 4:
                pe.wait_ge(s_wdone, u - 3)
            transpose_w(u)

        def transpose_x(b, chunks):
            pe.wait_ge(s_x, b * 16 + 16)
            for c in chunks:
                pe.wait_ge(s_xlo, b * DC + c + 1)
                for t in range(TPB):
                    last = nc.tensor.transpose(banks[:, c % 2, t * P:(t + 1) * P], x_in[:, t, c * P:(c + 1) * P], ident[:])
                last.then_inc(s_xT, 1)

        def norms_of(half, b):
            pe.wait_ge(s_sq, b * 2 * NG + (half + 1) * NG)
            pe.wait_ge(s_max, b * 2 + half + 1)
            for g in range(NG):
                last = nc.tensor.matmul(banks[HD * g:HD * g + HD, 6 + half, :], head_sum[:], squares[:, half * NG + g, :],
                                        start=True, stop=True)
            last.then_inc(s_norm, 1)

        transpose_x(0, range(DC))
        pe.wait_ge(s_wdone, 3 * DC)
        pe.wait_ge(s_hsum, G)
        with pe.Fori(0, NBLK // 2) as pair:
            for par in range(2):
                b = pair * 2 + par
                pe.wait_ge(s_xlo, b * DC + DC + 2)
                for j in range(NP):
                    if j < 4:
                        pe.wait_ge(s_hi, b * NP + j + 1)
                    else:
                        pe.wait_ge(s_lo, b * 2 * NG + j - 3)
                    for c in range(DC):
                        if j < 2 * NG:
                            m, g = divmod(j, NG)
                            cols = slice(g * P, (g + 1) * P)
                            parts = [(w_hi[:, m, c, cols], xT_hi[:, par, c, :]), (w_hi[:, m, c, cols], xT_lo[:, par, c, :]),
                                     (w_lo[:, m, c, cols], xT_hi[:, par, c, :])]
                        else:
                            cols = slice((j - 2 * NG) * P, (j - 2 * NG + 1) * P)
                            parts = [(xT_hi[:, par, c, cols], w_hi[:, 2, c, :]), (xT_hi[:, par, c, cols], w_lo[:, 2, c, :]),
                                     (xT_lo[:, par, c, cols], w_hi[:, 2, c, :])]
                        for i, (lhsT, rhs) in enumerate(parts):
                            last = nc.tensor.matmul(prod_bank[j % 4], lhsT, rhs, start=(c == 0 and i == 0),
                                                    stop=(c == DC - 1 and i == 2))
                    last.then_inc(s_prod, 1)
                    if j == NG + 1:
                        norms_of(0, b)
                    if j == NP - 3:
                        norms_of(1, b)
                    if j in X_STEPS:
                        transpose_x(b + 1, X_STEPS[j])
        pe.wait_ge(s_sign, 1)
        pe.wait_ge(s_hi, NBLK * NP + 4)
        for u in range(3 * DC, 4 * DC):
            transpose_w(u)
        pe.wait_ge(s_top, 1)
        for i in range(2):
            last = nc.tensor.transpose(banks[0:1, 0, i * P:(i + 1) * P], top[:, i:i + 1], ident[:])
        last.then_inc(s_topT, 1)
        pe.wait_ge(s_top, 3)
        nc.tensor.matmul(banks[:, 1, 0:1], ones_row[:], top_product[:], start=True, stop=True).then_inc(s_topT, 1)

    @block.scalar
    def _(act):
        act.sem_inc(s_hi, 4)
        for u in range(3 * DC):
            m, c = divmod(u, DC)
            act.wait_ge(s_wT, u + 1)
            nc.scalar.activation(w_hi[:, m, c, :], w_bank(u), ACT.Copy).then_inc(s_whi, 1)
        def split_x(b, par, chunks):
            for c in chunks:
                act.wait_ge(s_xT, b * DC + c + 1)
                nc.scalar.activation(xT_hi[:, par, c, :], banks[:, c % 2, :], ACT.Copy).then_inc(s_xhi, 1)

        split_x(0, 0, range(DC))
        with act.Fori(0, NBLK // 2) as pair:
            for par in range(2):
                b = pair * 2 + par
                for j in range(NP):
                    act.wait_ge(s_prod, b * NP + j + 1)
                    if j < 2 * NG:
                        if j == 0:
                            act.wait_ge(s_qst, b * 32 + 32)
                        if j == NG:
                            act.wait_ge(s_kst, b * 32 + 32)
                        nc.scalar.activation(qk_hi[:, j, :], prod_bank[j % 4], ACT.Copy).then_inc(s_hi, 1)
                        if j % NG == 0:
                            act.wait_ge(s_norm, b * 2 + j // NG + 1)
                        act.wait_ge(s_hi, b * NP + j + 1 + 4)
                        nc.scalar.activation(squares[:, j, :], qk_hi[:, j, :].bitcast(FP32), ACT.Square).then_inc(s_sq, 1)
                    else:
                        if j == 2 * NG:
                            act.wait_ge(s_vst, b * 16 + 16)
                        nc.scalar.activation(v_out[:, j - 2 * NG, :], prod_bank[j % 4], ACT.Copy).then_inc(s_hi, 1)
                    if j in X_STEPS:
                        split_x(b + 1, 1 - par, X_STEPS[j])
        act.wait_ge(s_top, 5)
        nc.scalar.activation(bound[:], bound_sq[:], ACT.Sqrt).then_inc(s_bound, 1)

    @block.vector
    def _(dve):
        dve.sem_inc(s_xlo, 2)
        dve.sem_inc(s_max, 2)
        dve.sem_inc(s_norm, 2)
        dve.sem_inc(s_qst, 32)
        dve.sem_inc(s_kst, 32)
        dve.sem_inc(s_vst, 16)
        for u in range(3 * DC):
            m, c = divmod(u, DC)
            dve.wait_ge(s_whi, u + 1)
            nc.vector.tensor_tensor(w_lo[:, m, c, :], w_bank(u), w_hi[:, m, c, :].bitcast(FP32), ALU.subtract).then_inc(s_wdone, 1)

        def split_x(b, par, chunks):
            for c in chunks:
                dve.wait_ge(s_xhi, b * DC + c + 1)
                nc.vector.tensor_tensor(xT_lo[:, par, c, :], banks[:, c % 2, :], xT_hi[:, par, c, :].bitcast(FP32),
                                        ALU.subtract).then_inc(s_xlo, 1)

        def largest(b, half):
            dve.wait_ge(s_norm, b * 2 + half + 1 + 2)
            nc.vector.reduce_max(norms[:, half, bass.ds(b, 1)], banks[:, 6 + half, :], AX.X).then_inc(s_max, 1)

        split_x(0, 0, range(DC))
        dve.wait_ge(s_w[3], 16)
        nc.vector.tensor_scalar(w_in[:, 3], w_in[:, 3], 0.0, 2.0, ALU.is_ge, ALU.mult).then_inc(s_sign, 1)
        dve.wait_ge(s_ffn, 48)
        dve.wait_ge(s_hsum, G + 3)
        nc.vector.tensor_copy(bias_rows[0:1, :], bias_in[0:1, :]).then_inc(s_bias, 1)
        nc.vector.tensor_copy(bias_rows[HD:HD + 1, :], bias_in[HD:HD + 1, :]).then_inc(s_bias, 1)
        dve.wait_ge(s_bias, 2)
        nc.vector.tensor_tensor(bias_rows[HD:HD + 1, :], bias_in[HD:HD + 1, :], bias_rows[HD:HD + 1, :].bitcast(FP32),
                                ALU.subtract).then_inc(s_bias, 1)
        with dve.Fori(0, NBLK // 2) as pair:
            for par in range(2):
                b = pair * 2 + par
                for j in range(2 * NG):
                    dve.wait_ge(s_hi, b * NP + j + 1 + 4)
                    nc.vector.tensor_tensor(qk_lo[:, j, :], prod_bank[j % 4], qk_hi[:, j, :].bitcast(FP32),
                                            ALU.subtract).then_inc(s_lo, 1)
                first, second = X_STEPS.values()
                split_x(b + 1, 1 - par, first)
                largest(b, 0)
                largest(b, 1)
                split_x(b + 1, 1 - par, second)
        dve.wait_ge(s_max, 2 * NBLK + 2)
        nc.vector.reduce_max(top[:], norms[:], AX.X).then_inc(s_top, 1)
        dve.wait_ge(s_topT, 1)
        nc.vector.reduce_max(top_both[:], banks[0:1, 0, 0:2 * P].rearrange("o (i p) -> o i p", i=2), AX.X).then_inc(s_top, 1)
        dve.wait_ge(s_top, 2)
        nc.vector.tensor_tensor(top_product[:], top_both[:, 0:1], top_both[:, 1:2], ALU.mult).then_inc(s_top, 1)
        dve.wait_ge(s_topT, 2)
        nc.vector.tensor_scalar(flag[:], banks[0:1, 1, 0:1], BOUND_SLACK, BOUND_SQ_MAX, ALU.mult, ALU.is_gt).then_inc(s_top, 1)
        nc.vector.tensor_scalar(bound_sq[:], banks[:, 1, 0:1], BOUND_SLACK, BOUND_SQ_MAX, ALU.mult, ALU.min).then_inc(s_top, 1)
        dve.wait_ge(s_bound, 1)
        nc.vector.tensor_scalar(bound[:], bound[:], -SHIFT, None, ALU.mult).then_inc(s_top, 1)
        dve.wait_ge(s_top, 6)
        dve.wait_ge(s_const, 5)
        nc.vector.tensor_scalar(shift_rows[:], zero_rows[:], bound[0:N * H, :], None, ALU.add).then_inc(s_top, 1)
        for c in range(DC):
            dve.wait_ge(s_wT, 3 * DC + c + 1)
            nc.vector.scalar_tensor_tensor(out=wf_scaled[:, c, :], in0=w_bank(3 * DC + c), scalar=-1.0, in1=scale_b[:],
                                           op0=ALU.add, op1=ALU.mult).then_inc(s_scaled, 1)


def exact_maxima(nc, ctx, dram, banks, inputs):
    load_q, _, load_k, load_v = inputs[-4:]

    def sb(name, shape, dt):
        return ctx.enter_context(nc.sbuf_tensor(name, shape, dt))

    def sem(name):
        return ctx.enter_context(nc.semaphore(name))

    q_head = sb("q_head", [3 * HD, S], FP32R)
    k_head = sb("k_head", [3 * HD, S], FP32R)
    maxima = sb("maxima", [P, KT], FP32)
    max_hi = sb("max_hi", [KT, P], FP32R)
    max_lo = sb("max_lo", [KT, P], FP32R)
    ident2 = sb("ident2", [P, P], FP32)
    flag = dram["flag"]

    m_id = sem("m_id")
    m_load = sem("m_load")
    m_score = sem("m_score")
    m_max = sem("m_max")
    m_T = sem("m_T")
    m_hi = sem("m_hi")
    m_lo = sem("m_lo")
    m_store = sem("m_store")

    block = ctx.enter_context(nc.Block())

    @block.sync
    def _(sp):
        load_q(sp, 0, 0)
        load_k(sp, 0, 0)
        load_v(sp, 0, 0, 0)
        needed = sp.value_load(flag[0:1, 0:1])
        with sp.If(needed > 0):
            with sp.Fori(0, N * H) as h:
                sp.wait_ge(m_store, h * 32 + 32)
                for r, (qs, ks) in enumerate((("q_hi", "k_hi"), ("q_lo", "k_hi"), ("q_hi", "k_lo"))):
                    for dst, src in ((q_head, qs), (k_head, ks)):
                        rows = dram[src].rearrange("n (h r) t -> (n h) r t", r=HD)[bass.ds(h, 1)]
                        sp.dma_start(dst[HD * r:HD * r + HD, :].bitcast(FP32), rows.rearrange("o r t -> (o r) t")).then_inc(m_load, 16)
                sp.wait_ge(m_lo, h + 2)
                for part, src in ((0, max_hi), (1, max_lo)):
                    row = dram["shift"][part][bass.ds(h, 1)].rearrange("o (t p) -> (o t) p", p=P)
                    sp.dma_start(row, src[:].bitcast(FP32)).then_inc(m_store, 16)
            sp.wait_ge(m_store, 32 * N * H + 32)

    @block.gpsimd
    def _(pool):
        nc.gpsimd.memset(ident2[:], 0.0).then_inc(m_id, 1)
        pool.wait_ge(m_id, 1)
        nc.gpsimd.affine_select(out=ident2[:], in_=ident2[:], compare_op=ALU.not_equal, fill=1.0, base=0,
                                pattern=[[-1, P]], channel_multiplier=1).then_inc(m_id, 1)
        pool.sem_inc(m_store, 32)
        pool.sem_inc(m_max, 2)
        pool.sem_inc(m_lo, 1)

    @block.tensor
    def _(pe):
        needed = pe.value_load(flag[0:1, 0:1])
        with pe.If(needed > 0):
            pe.wait_ge(m_id, 2)
            with pe.Fori(0, N * H) as h:
                pe.wait_ge(m_load, h * 96 + 96)
                for t in range(KT):
                    pe.wait_ge(m_max, h * KT + t + 1)
                    if t == 0:
                        pe.wait_ge(m_lo, h + 1)
                    for kb in range(QB):
                        last = nc.tensor.matmul(banks[:, 4 * (t % 2) + kb, :], q_head[:, t * P:(t + 1) * P],
                                                k_head[:, kb * BLK:(kb + 1) * BLK], start=True, stop=True)
                    last.then_inc(m_score, 1)
                pe.wait_ge(m_max, h * KT + KT + 2)
                nc.tensor.transpose(banks[0:KT, 0, 0:P], maxima[:], ident2[:]).then_inc(m_T, 1)

    @block.vector
    def _(dve):
        needed = dve.value_load(flag[0:1, 0:1])
        with dve.If(needed > 0):
            with dve.Fori(0, N * H) as h:
                for t in range(KT):
                    dve.wait_ge(m_score, h * KT + t + 1)
                    nc.vector.reduce_max(maxima[:, t:t + 1], banks[:, 4 * (t % 2):4 * (t % 2) + 4, :]
                                         .rearrange("p b k -> p (b k)"), AX.X).then_inc(m_max, 1)
                dve.wait_ge(m_T, h + 1)
                dve.wait_ge(m_store, h * 32 + 32)
                nc.vector.tensor_scalar(max_hi[:], banks[0:KT, 0, 0:P], -1.0, None, ALU.mult).then_inc(m_hi, 1)
                dve.wait_ge(m_hi, h + 1)
                nc.vector.scalar_tensor_tensor(out=max_lo[:], in0=banks[0:KT, 0, 0:P], scalar=-1.0, in1=max_hi[:].bitcast(FP32),
                                               op0=ALU.mult, op1=ALU.subtract).then_inc(m_lo, 1)


def attention_inputs(nc, ctx, dram):

    def sb(name, shape, dt):
        return ctx.enter_context(nc.sbuf_tensor(name, shape, dt))

    def sem(name):
        return ctx.enter_context(nc.semaphore(name))

    q_rows = sb("q_rows", [KROWS, G, S], FP32R)
    k_rows = sb("k_rows", [KROWS, G, S], FP32R)
    v_keys = sb("v_keys", [P, KT, P], FP32)
    a_q = [sem(f"a_q{c}") for c in range(QB)]
    a_k = [sem(f"a_k{c}") for c in range(QB)]

    v_src = dram["v"].rearrange("(n b) (t p) (g d) -> n g b p t d", n=N, p=P, g=NG)

    def load_q(sp, it, c):
        cols = slice(c * BLK, (c + 1) * BLK)
        for r, part in enumerate(("q_hi", "q_lo", "q_hi")):
            src = dram[part].rearrange("n (g h r) t -> (n g) r h t", g=NG, r=HD)[bass.ds(it, 1), :, :, cols]
            sp.dma_start(q_rows[HD * r:HD * r + HD, :, cols].bitcast(FP32), src.rearrange("o r h t -> (o r) h t")).then_inc(a_q[c], 16)

    def load_shift(sp, it, c):
        cols = slice(c * BLK, (c + 1) * BLK)
        src = dram["shift"].rearrange("s (i h) t -> i s h t", h=G)[bass.ds(it, 1), :, :, cols]
        sp.dma_start(q_rows[3 * HD:KROWS, :, cols].bitcast(FP32), src.rearrange("o s h t -> (o s) h t")).then_inc(a_q[c], 16)

    def load_k(sp, it, c):
        cols = slice(c * BLK, (c + 1) * BLK)
        for r, part in enumerate(("k_hi", "k_hi", "k_lo")):
            src = dram[part].rearrange("n (g h r) t -> (n g) r h t", g=NG, r=HD)[bass.ds(it, 1), :, :, cols]
            sp.dma_start(k_rows[HD * r:HD * r + HD, :, cols].bitcast(FP32), src.rearrange("o r h t -> (o r) h t")).then_inc(a_k[c], 16)

    def load_v(sp, n, g, c):
        src = v_src[bass.ds(n, 1), bass.ds(g, 1), c].rearrange("o u p t d -> p (o u t) d")
        sp.dma_start(v_keys[:, c * TPB:(c + 1) * TPB, :], src).then_inc(a_k[c], 16)

    return q_rows, k_rows, v_keys, a_q, a_k, load_q, load_shift, load_k, load_v


def attend(nc, ctx, dram, banks, ffn, inputs, first):

    wf_hi, wf_lo, _, _, wf_scaled = ffn
    q_rows, k_rows, v_keys, a_q, a_k, load_q, load_shift, load_k, load_v = inputs

    def sb(name, shape, dt):
        return ctx.enter_context(nc.sbuf_tensor(name, shape, dt))

    def sem(name):
        return ctx.enter_context(nc.semaphore(name))

    probs = sb("probs", [P, P_RING, G, BLK], FP32)
    sums = sb("sums", [P, 2, CHAINS, G, BLK], FP32)
    ones = sb("ones", [P, HD], FP32)
    out_sb, den_sb = wf_scaled[:, 0:2, :], wf_scaled[:, 2:4, :]

    a_wfhi = sem("a_wfhi")
    a_wflo = sem("a_wflo")
    a_one = sem("a_one")
    a_score = sem("a_score")
    a_prob = sem("a_prob")
    a_pv = sem("a_pv")
    a_sum = sem("a_sum")
    a_order = sem("a_order")
    a_merge = sem("a_merge")
    a_den = sem("a_den")
    a_out = sem("a_out")
    a_dout = sem("a_dout")
    a_store = [sem(f"a_store{h}") for h in range(2)]

    UNITS = 2 * KT
    STEP_Q = 4 * 16
    STEP_K = 4 * 16

    ITEM_UNITS = QB * UNITS
    LAST = ITEMS - 1

    def scores_of(unit):
        return banks[:, 2 * (unit % SLOTS):2 * (unit % SLOTS) + 2, :]

    def slot_before(unit):
        return unit - SLOTS if unit >= SLOTS else max(v for v in range(ITEM_UNITS) if v % SLOTS == unit) - ITEM_UNITS

    def out_bank(qb):
        return 2 * SLOTS + qb % 2

    block = ctx.enter_context(nc.Block())

    @block.sync
    def _(sp):
        def store(it, qb):
            cols = slice(qb * BLK, (qb + 1) * BLK)
            sp.wait_ge(a_out, it * QB + qb + 1)
            dst = dram["attn"].rearrange("n (g p) t -> (n g) p t", p=P)[bass.ds(it, 1), :, cols]
            sp.dma_start(dst.rearrange("o p t -> (o p) t"), out_sb[:, qb % 2, :]).then_inc(a_store[qb % 2], 16)
            sp.wait_ge(a_dout, it * QB + qb + 1 + 2)
            dst = dram["den"].rearrange("(i h) t -> i h t", h=G)[bass.ds(it, 1), :, cols]
            sp.dma_start(dst.rearrange("o h t -> (o h) t"), den_sb[0:P:HD, qb % 2, :]).then_inc(a_store[qb % 2], 16)

        load_shift(sp, 0, 0)
        for c in range(1, QB):
            load_k(sp, 0, c)
            load_v(sp, 0, 0, c)
        for c in range(1, QB):
            load_q(sp, 0, c)
            load_shift(sp, 0, c)
        with sp.Fori(0, LAST) as it:
            ahead = sp.snap(it + 1)
            n_ahead = sp.snap((it + 1) // NG)
            g_ahead = sp.snap((it + 1) % NG)
            for qb in range(QB):
                st = it * QB + qb
                if qb == QB - 1:
                    for c in range(QB):
                        sp.wait_ge(a_score, st * UNITS + 2 * TPB * (c + 1))
                        load_k(sp, ahead, c)
                        if c > 0:
                            sp.wait_ge(a_pv, st * KT + TPB * c + P_RING)
                            load_v(sp, n_ahead, g_ahead, c - 1)
                        if c == 2:
                            store(it, qb - 1)
                sp.wait_ge(a_score, st * UNITS + UNITS)
                load_q(sp, ahead, qb)
                load_shift(sp, ahead, qb)
                if 0 < qb < QB - 1:
                    store(it, qb - 1)
            sp.wait_ge(a_pv, (it * QB + QB) * KT + P_RING)
            load_v(sp, n_ahead, g_ahead, QB - 1)
            store(it, QB - 1)
        for h in range(2):
            sp.wait_ge(a_store[h], (LAST * QB // 2) * 32 + 32)
        attn_first, den_first, first_in = first
        sp.dma_start(attn_first[:], dram["attn"][0, :, 0:BLK].rearrange("(c p) t -> p c t", p=P)).then_inc(first_in, 16)
        sp.dma_start(den_first[:], dram["den"][0:H, 0:BLK]).then_inc(first_in, 16)
        for qb in range(QB):
            store(LAST, qb)
        for h in range(2):
            sp.wait_ge(a_store[h], ITEMS * QB // 2 * 32 + 32)

    @block.gpsimd
    def _(pool):
        nc.gpsimd.memset(ones[:], 1.0).then_inc(a_one, 1)
        pool.wait_ge(a_one, 1)
        for c in range(QB):
            nc.gpsimd.memset(k_rows[3 * HD:KROWS, :, c * BLK:(c + 1) * BLK].bitcast(FP32), 1.0).then_inc(a_one, 1)

        def merge(it, qb):
            pool.wait_ge(a_sum, ((it * QB + qb) + 1) * KT + P_RING)
            pool.sem_inc(a_order, 1)
            pool.dma_start(sums[:, qb % 2, 0], sums[:, qb % 2, 1], accum_op=ALU.add).then_inc(a_merge, 16)

        with pool.Fori(0, LAST) as it:
            for qb in range(QB):
                merge(it, qb)
        for qb in range(QB - 1):
            merge(LAST, qb)

    @block.tensor
    def _(pe):
        pe.sem_inc(a_pv, P_RING)
        pe.sem_inc(a_den, 2)

        def scores(it, qb, kt):
            st = it * QB + qb
            if kt == 0:
                pe.wait_ge(a_q[qb], it * STEP_Q + STEP_Q)
            if qb == 0 and kt % TPB == 0:
                pe.wait_ge(a_k[kt // TPB], it * STEP_K + STEP_K)
                pe.wait_ge(a_one, kt // TPB + 2)
            for half in range(2):
                unit = qb * UNITS + 2 * kt + half
                pe.wait_ge(a_prob, it * ITEM_UNITS + slot_before(unit) + 1 + SLOTS)
                for i in range(2):
                    h = 2 * half + i
                    last = nc.tensor.matmul(scores_of(unit)[:, i, :], k_rows[:, h, kt * P:(kt + 1) * P],
                                            q_rows[:, h, qb * BLK:(qb + 1) * BLK], start=True, stop=True)
                last.then_inc(a_score, 1)

        def values(it, qb, kt):
            st = it * QB + qb
            pe.wait_ge(a_prob, st * UNITS + 2 * kt + 2 + SLOTS)
            if kt == 0:
                pe.wait_ge(a_dout, st + 1)
            for h in range(G):
                rows = slice(HD * h, HD * h + HD)
                last = nc.tensor.matmul(banks[rows, out_bank(qb), :], v_keys[:, kt, rows], probs[:, kt % P_RING, h, :],
                                        start=(kt == 0), stop=(kt == KT - 1))
            last.then_inc(a_pv, 1)

        def denominators(it, qb):
            st = it * QB + qb
            if it is LAST and qb == QB - 1:
                pe.wait_ge(a_sum, (st + 1) * KT + P_RING)
                chains = CHAINS
            else:
                pe.wait_ge(a_merge, st * 16 + 16)
                chains = 1
            pe.wait_ge(a_out, st + 1)
            for chain in range(chains):
                for h in range(G):
                    rows = slice(HD * h, HD * h + HD)
                    last = nc.tensor.matmul(banks[rows, out_bank(qb), :], ones[:], sums[:, qb % 2, chain, h, :],
                                            start=(chain == 0), stop=(chain == chains - 1))
            last.then_inc(a_den, 1)

        def steps(it, qb, tiles):
            for kt in tiles:
                if kt + LAG < KT:
                    scores(it, qb, kt + LAG)
                elif qb < QB - 1:
                    scores(it, qb + 1, kt + LAG - KT)
                elif it is not LAST:
                    scores(it + 1, 0, kt + LAG - KT)
                values(it, qb, kt)
                if kt == DEN_TILE and qb > 0:
                    denominators(it, qb - 1)

        def item(it):
            steps(it, 0, range(HEAD, KT))
            for qb in range(1, QB):
                steps(it, qb, range(KT))
            if it is not LAST:
                steps(it + 1, 0, range(HEAD))
            denominators(it, QB - 1)

        HEAD = DEN_TILE + 1
        for kt in range(LAG):
            scores(0, 0, kt)
        steps(0, 0, range(HEAD))
        with pe.Fori(0, ITEMS - 1) as it:
            item(it)
        item(LAST)

    @block.scalar
    def _(act):
        act.sem_inc(a_prob, SLOTS)
        act.sem_inc(a_dout, 2)

        nc.scalar.activation(wf_hi[:], wf_scaled[:], ACT.Copy).then_inc(a_wfhi, 1)

        def copy_out(st, parity):
            act.wait_ge(a_wflo, 1)
            act.wait_ge(a_pv, st * KT + KT + P_RING)
            act.wait_ge(a_store[parity], (st - parity) * 16 + 32)
            nc.scalar.activation(out_sb[:, parity, :], banks[:, out_bank(parity), :], ACT.Copy).then_inc(a_out, 1)

        def copy_den(st, parity):
            act.wait_ge(a_den, st + 1 + 2)
            act.wait_ge(a_store[parity], (st - parity) * 16 + 32)
            nc.scalar.activation(den_sb[:, parity, :], banks[:, out_bank(parity), :], ACT.Copy).then_inc(a_dout, 1)

        def item(it, first):
            for qb in range(QB):
                st = it * QB + qb
                for u in range(UNITS):
                    kt, half = divmod(u, 2)
                    act.wait_ge(a_score, st * UNITS + u + 1)
                    before = kt - P_RING if kt >= P_RING else max(v for v in range(KT) if v % P_RING == kt) - KT
                    if half == 0:
                        act.wait_ge(a_pv, st * KT + before + 1 + P_RING)
                        act.wait_ge(a_sum, st * KT + before + 1 + P_RING)
                    heads = slice(2 * half, 2 * half + 2)
                    nc.scalar.activation(probs[:, kt % P_RING, heads, :], scores_of(qb * UNITS + u), ACT.Exp,
                                         scale=SCALE).then_inc(a_prob, 1)
                    if u == 2 * LAG - 1 and not (first and qb == 0):
                        copy_out(st - 1, (qb - 1) % 2)
                    if u == 2 * (LAG + DEN_TILE) + 1 and not (first and qb == 0):
                        copy_den(st - 1, (qb - 1) % 2)

        item(0, True)
        with act.Fori(1, ITEMS) as it:
            item(it, False)
        copy_out(ITEMS * QB - 1, 1)
        copy_den(ITEMS * QB - 1, 1)

    @block.vector
    def _(dve):
        dve.wait_ge(a_wfhi, 1)
        nc.vector.tensor_tensor(wf_lo[:], wf_scaled[:], wf_hi[:].bitcast(FP32), ALU.subtract).then_inc(a_wflo, 1)
        dve.sem_inc(a_sum, P_RING)
        dve.sem_inc(a_store[0], 32)
        dve.sem_inc(a_store[1], 32)

        with dve.Fori(0, ITEMS) as it:
            for qb in range(QB):
                st = it * QB + qb
                for kt in range(CHAINS, KT):
                    total = sums[:, qb % 2, kt % CHAINS]
                    dve.wait_ge(a_prob, st * UNITS + 2 * kt + 2 + SLOTS)
                    if kt < 2 * CHAINS:
                        dve.wait_ge(a_den, st + 1)
                        freed = 1 if kt < 2 * CHAINS - 1 else CHAINS + 1
                        nc.vector.tensor_tensor(total, probs[:, kt - CHAINS], probs[:, kt], ALU.add).then_inc(a_sum, freed)
                    else:
                        dve.wait_ge(a_sum, st * KT + (kt - CHAINS + 1 if kt >= 3 * CHAINS - 1 else kt - 2 * CHAINS + 1) + P_RING)
                        nc.vector.tensor_tensor(total, total, probs[:, kt % P_RING], ALU.add).then_inc(a_sum, 1)


def normalise_and_ffn(nc, ctx, dram, x, ffn, first, banks, out):
    wf_hi, wf_lo, bias_ones, bias_rows, _ = ffn

    def sb(name, shape, dt):
        return ctx.enter_context(nc.sbuf_tensor(name, shape, dt))

    def sem(name):
        return ctx.enter_context(nc.semaphore(name))

    PERIOD = 2 * TPB
    TILES = N * S // P
    ROUNDS = TILES // PERIOD
    Y_SLOTS = 8
    ident3 = sb("ident3", [P, P], FP32)
    eps = sb("eps", [P, 1], FP32)
    x_in = sb("x_res", [P, 2, TPB, D], FP32)
    attnT = [first[0], sb("attnT1", [P, DC, BLK], FP32)]
    den_in = [first[1], sb("den_in1", [H, BLK], FP32)]
    rden = sb("rden", [P, 2, H], FP32)
    attn = sb("attn", [P, 2, D], FP32)
    res1 = sb("res1", [P, 2, D], FP32)
    y = sb("y", [P, Y_SLOTS, D], FP32)
    yT_hi = sb("yT_hi", [P, 4, D], FP32R)
    yT_lo = sb("yT_lo", [P, 4, D], FP32R)
    clipped = sb("clipped", [P, 2, D], FP32)
    res2 = sb("res2", [P, 2, D], FP32)
    y2 = sb("y2", [P, 4, D], FP32)
    stats = sb("stats", [P, 2, 2, 6], FP32)
    mean_var = sb("mean_var", [P, 2, 2, 2], FP32)
    std = sb("std", [P, 2, 2, 1], FP32)
    rstd = sb("rstd", [P, 2, 2, 1], FP32)
    offset = sb("offset", [P, 2, 2, 1], FP32)

    f_const = sem("f_const")
    f_in = [first[2], sem("f_in1")]
    f_x = [sem(f"f_x{k}") for k in range(2)]
    f_aT = sem("f_aT")
    f_rden = sem("f_rden")
    f_attn = sem("f_attn")
    f_res = [sem("f_res1"), sem("f_res2")]
    f_stat = [sem("f_stat1"), sem("f_stat2")]
    f_order = sem("f_order")
    f_std = [sem("f_std1"), sem("f_std2")]
    f_rstd = [sem("f_rstd1"), sem("f_rstd2")]
    f_y = [sem("f_y1"), sem("f_y2")]
    f_yT = sem("f_yT")
    f_yhi = sem("f_yhi")
    f_ylo = sem("f_ylo")
    f_ffn = sem("f_ffn")
    f_clip = sem("f_clip")
    f_out = [sem(f"f_out{k}") for k in range(4)]

    def aT_bank(s):
        return banks[:, s % 2, :]

    def den_bank(s):
        return banks[:, 6 + s % 2, 0:H]

    def yT_bank(s):
        return banks[:, 2 + s % 2, :]

    def ffn_bank(s):
        return banks[:, 4 + s % 2, :]

    ATTN, LN1, TRANS, FFN, CLIP, LN2 = 0, 1, 2, 4, 5, 6

    def tile(r, j, lag):
        if isinstance(r, int) and not 0 <= r * PERIOD + j - lag < TILES:
            return None, None
        return r * PERIOD + (j - lag), (j - lag) % PERIOD

    def all_steps(engine, step):
        for j in range(PERIOD):
            step(0, j)
        with engine.Fori(1, ROUNDS) as r:
            for j in range(PERIOD):
                step(r, j)
        for j in range(LN2):
            step(ROUNDS, j)

    block = ctx.enter_context(nc.Block())

    @block.sync
    def _(sp):
        def load_x(b, k):
            sp.dma_start(x_in[:, k], x[bass.ds(b, 1)].rearrange("o p t d -> p (o t) d")).then_inc(f_x[k], 16)

        def load(b, batch, column, k):
            sp.wait_ge(f_res[0], b * TPB + TPB)
            src = dram["attn"][bass.ds(batch, 1), :, bass.ds(column, BLK)]
            sp.dma_start(attnT[k][:], src.rearrange("o (c p) t -> p (o c) t", p=P)).then_inc(f_in[k], 16)
            src = dram["den"].rearrange("(n h) t -> n h t", n=N)[bass.ds(batch, 1), :, bass.ds(column, BLK)]
            sp.dma_start(den_in[k][:], src.rearrange("o h t -> (o h) t")).then_inc(f_in[k], 16)
            load_x(b, k)

        load_x(0, 0)
        with sp.Fori(0, ROUNDS - 1) as r:
            blocks = [sp.snap(r * 2 + 1 + i) for i in range(2)]
            batches = [sp.snap((r * 2 + 1 + i) // QB) for i in range(2)]
            columns = [sp.snap((r * 2 + 1 + i) % QB * BLK) for i in range(2)]
            for i in range(2):
                load(blocks[i], batches[i], columns[i], (1 + i) % 2)
        load(NBLK - 1, N - 1, (QB - 1) * BLK, 1)

    @block.gpsimd
    def _(pool):
        nc.gpsimd.memset(ident3[:], 0.0).then_inc(f_const, 1)
        nc.gpsimd.memset(eps[:], EPS).then_inc(f_const, 1)
        pool.sem_inc(f_res[0], 2 * TPB)
        pool.sem_inc(f_res[1], Y_SLOTS)
        pool.wait_ge(f_const, 2)
        nc.gpsimd.affine_select(out=ident3[:], in_=ident3[:], compare_op=ALU.not_equal, fill=1.0, base=0,
                                pattern=[[-1, P]], channel_multiplier=1).then_inc(f_const, 1)

        def step(r, j):
            t, s = tile(r, j, CLIP)
            if t is not None:
                pool.wait_ge(f_clip, t + 1 + 2)
                pool.wait_ge(f_y[1], t + 1)
                nc.gpsimd.tensor_tensor(res2[:, s % 2], clipped[:, s % 2], y[:, s % Y_SLOTS], ALU.add).then_inc(f_res[1], 1)
            t, s = tile(r, j, ATTN)
            if t is not None:
                if s % TPB == 0:
                    pool.wait_ge(f_x[s // TPB], r * 16 + 16)
                pool.wait_ge(f_attn, t + 1 + 2)
                pool.wait_ge(f_y[0], t + 1)
                nc.gpsimd.tensor_tensor(res1[:, s % 2], attn[:, s % 2], x_in[:, s // TPB, s % TPB], ALU.add).then_inc(f_res[0], 1)

        all_steps(pool, step)

    @block.tensor
    def _(pe):
        pe.sem_inc(f_ffn, 4)
        pe.wait_ge(f_const, 3)

        def step(r, j):
            t, s = tile(r, j, ATTN)
            if t is not None:
                k = s // TPB
                cols = slice(s % TPB * P, (s % TPB + 1) * P)
                if s % TPB == 0:
                    pe.wait_ge(f_in[k], r * 32 + 32)
                pe.wait_ge(f_attn, t + 1)
                for c in range(DC):
                    nc.tensor.transpose(aT_bank(s)[:, c * P:(c + 1) * P], attnT[k][:, c, cols], ident3[:])
                nc.tensor.transpose(den_bank(s), den_in[k][:, cols], ident3[0:H, 0:H]).then_inc(f_aT, 1)
            t, s = tile(r, j, TRANS)
            if t is not None:
                pe.wait_ge(f_y[0], t + 1 + 2)
                pe.wait_ge(f_ylo, t + 1)
                for c in range(DC):
                    last = nc.tensor.transpose(yT_bank(s)[:, c * P:(c + 1) * P], y[:, s % Y_SLOTS, c * P:(c + 1) * P], ident3[:])
                last.then_inc(f_yT, 1)
            t, s = tile(r, j, FFN)
            if t is not None:
                pe.wait_ge(f_ylo, t + 1 + 2)
                pe.wait_ge(f_clip, t + 1)
                nc.tensor.matmul(ffn_bank(s), bias_ones[:], bias_rows[:], start=True, stop=False)
                for c in range(DC):
                    cols = slice(c * P, (c + 1) * P)
                    for part, w in ((yT_hi, wf_hi), (yT_lo, wf_hi), (yT_hi, wf_lo)):
                        last = nc.tensor.matmul(ffn_bank(s), part[:, s % 4, cols], w[:, c, :], start=False,
                                                stop=(c == DC - 1 and w is wf_lo))
                last.then_inc(f_ffn, 1)

        all_steps(pe, step)

    @block.scalar
    def _(act):
        act.sem_inc(f_y[0], 2)
        act.sem_inc(f_y[1], 2)

        def deviation(t, s, which):
            act.wait_ge(f_stat[which], (t + 1) * 2)
            act.wait_ge(f_rstd[which], (t + 1) * 2)
            nc.scalar.activation(std[:, s % 2, which], mean_var[:, s % 2, which, 1:2], ACT.Sqrt, bias=eps[:]).then_inc(f_std[which], 1)

        def layernorm(t, s, which, src, dst, slots):
            act.wait_ge(f_rstd[which], (t + 1) * 2 + 4)
            nc.scalar.activation(dst[:, s % slots], src[:, s % 2], ACT.Identity, scale=rstd[:, s % 2, which],
                                 bias=offset[:, s % 2, which]).then_inc(f_y[which], 1)

        act.wait_ge(f_const, 2)

        def step(r, j):
            t, s = tile(r, j, LN1)
            if t is not None:
                deviation(t, s, 0)
            t, s = tile(r, j, LN2)
            if t is not None:
                deviation(t, s, 1)
            t, s = tile(r, j, TRANS)
            if t is not None:
                act.wait_ge(f_yT, t + 1)
                act.wait_ge(f_ffn, t + 1)
                nc.scalar.activation(yT_hi[:, s % 4], yT_bank(s), ACT.Copy).then_inc(f_yhi, 1)
            t, s = tile(r, j, LN1)
            if t is not None:
                act.wait_ge(f_res[1], t + 1)
                layernorm(t, s, 0, res1, y, Y_SLOTS)
            t, s = tile(r, j, LN2)
            if t is not None:
                act.wait_ge(f_out[s % 4], (r * (PERIOD // 4) + (j - LN2) // 4) * 16 + 16)
                layernorm(t, s, 1, res2, y2, 4)
                row = t if isinstance(t, int) else act.snap(t)
                act.wait_ge(f_y[1], t + 1 + 2)
                act.dma_start(out[bass.ds(row, 1)].rearrange("o p d -> (o p) d"), y2[:, s % 4]).then_inc(f_out[s % 4], 16)

        all_steps(act, step)
        for k in range(4):
            act.wait_ge(f_out[k], TILES // 4 * 16 + 16)

    @block.vector
    def _(dve):
        dve.sem_inc(f_attn, 2)
        dve.sem_inc(f_ylo, 2)
        dve.sem_inc(f_clip, 2)
        for which in range(2):
            dve.sem_inc(f_rstd[which], 4)
        for k in range(4):
            dve.sem_inc(f_out[k], 16)

        def statistics(t, s, which, src, credit):
            dve.wait_ge(f_res[which], t + 1 + credit)
            nc.vector.bn_stats(stats[:, s % 2, which], src[:, s % 2]).then_inc(f_stat[which], 1)

        def aggregate(t, s, which):
            dve.wait_ge(f_stat[which], t * 2 + 1)
            dve.sem_inc(f_order, 1)
            nc.vector.bn_aggr(mean_var[:, s % 2, which], stats[:, s % 2, which]).then_inc(f_stat[which], 1)

        def reciprocal_std(t, s, which):
            dve.wait_ge(f_std[which], t + 1)
            dve.wait_ge(f_y[which], t + 1)
            nc.vector.reciprocal(rstd[:, s % 2, which], std[:, s % 2, which]).then_inc(f_rstd[which], 1)

        def offset_of(t, s, which):
            dve.wait_ge(f_rstd[which], t * 2 + 1 + 4)
            nc.vector.scalar_tensor_tensor(out=offset[:, s % 2, which], in0=mean_var[:, s % 2, which, 0:1], scalar=-1.0,
                                           in1=rstd[:, s % 2, which], op0=ALU.mult, op1=ALU.mult).then_inc(f_rstd[which], 1)

        def step(r, j):
            norms = [(*tile(r, j, lag), which) for lag, which in ((LN1, 0), (LN2, 1))]
            norms = [(t, s, which) for t, s, which in norms if t is not None]
            t, s = tile(r, j, CLIP)
            if t is not None:
                dve.wait_ge(f_ffn, t + 1 + 4)
                dve.wait_ge(f_res[1], t + 1 - 2 + Y_SLOTS)
                nc.vector.tensor_scalar(clipped[:, s % 2], ffn_bank(s), -MAX_VAL, MAX_VAL, ALU.max, ALU.min).then_inc(f_clip, 1)
            for t, s, which in norms:
                statistics(t, s, which, (res1, res2)[which], (2 * TPB, Y_SLOTS)[which])
            attn_t, attn_s = tile(r, j, ATTN)
            if attn_t is not None:
                dve.wait_ge(f_aT, attn_t + 1)
                dve.wait_ge(f_attn, attn_t + 1)
                nc.vector.reciprocal(rden[:, attn_s % 2], den_bank(attn_s)).then_inc(f_rden, 1)
            for t, s, which in norms:
                aggregate(t, s, which)
            if attn_t is not None:
                dve.wait_ge(f_rden, attn_t + 1)
                dve.wait_ge(f_res[0], attn_t + 1 - 2 + 2 * TPB)
                nc.vector.tensor_tensor(attn[:, attn_s % 2].rearrange("p (h d) -> p h d", h=H),
                                        aT_bank(attn_s).rearrange("p (h d) -> p h d", h=H),
                                        rden[:, attn_s % 2].unsqueeze(2).to_broadcast([P, H, HD]), ALU.mult).then_inc(f_attn, 1)
            for t, s, which in norms:
                reciprocal_std(t, s, which)
            for t, s, which in norms:
                offset_of(t, s, which)
            t, s = tile(r, j, TRANS)
            if t is not None:
                dve.wait_ge(f_yhi, t + 1)
                nc.vector.tensor_tensor(yT_lo[:, s % 4], yT_bank(s), yT_hi[:, s % 4].bitcast(FP32), ALU.subtract).then_inc(f_ylo, 1)

        all_steps(dve, step)


def build(nc, x, Wq, Wk, Wv, Wf, scale, bias, out):
    def scratch(name, shape, dt):
        return nc.dram_tensor("scratch_" + name, shape, dt, kind="Internal").ap()

    x_blocks = x.rearrange("n (b t p) d -> (n b) p t d", p=P, t=TPB)
    out_tiles = out.rearrange("n (t p) d -> (n t) p d", p=P)
    dram = {k: scratch(k, (N, D, S), FP32) for k in ("q_hi", "q_lo", "k_hi", "k_lo")}
    dram["v"] = scratch("v", (NBLK, BLK, D), FP32)
    dram["shift"] = scratch("shift", (2, N * H, S), FP32)
    dram["attn"] = scratch("attn", (N, D, S), FP32)
    dram["den"] = scratch("den", (N * H, S), FP32)
    with ExitStack() as whole:
        banks = whole.enter_context(nc.psum_tensor("banks", [P, 8, BLK], FP32))
        ffn = [whole.enter_context(nc.sbuf_tensor(name, shape, FP32R)) for name, shape in (
            ("wf_hi", [P, DC, D]), ("wf_lo", [P, DC, D]), ("bias_ones", [2 * HD, P]), ("bias_rows", [2 * HD, D]))]
        ffn.append(whole.enter_context(nc.sbuf_tensor("wf_scaled", [P, DC, D], FP32)))
        dram["flag"] = whole.enter_context(nc.sbuf_tensor("flag", [1, 1], INT32))
        with ExitStack() as ctx:
            project(nc, ctx, dram, (x_blocks, Wq, Wk, Wv, Wf, scale, bias), banks, ffn)
        first = (whole.enter_context(nc.sbuf_tensor("attnT0", [P, DC, BLK], FP32)),
                 whole.enter_context(nc.sbuf_tensor("den_in0", [H, BLK], FP32)), whole.enter_context(nc.semaphore("f_in0")))
        with ExitStack() as both:
            inputs = attention_inputs(nc, both, dram)
            with ExitStack() as ctx:
                exact_maxima(nc, ctx, dram, banks, inputs)
            with ExitStack() as ctx:
                attend(nc, ctx, dram, banks, ffn, inputs, first)
        with ExitStack() as ctx:
            normalise_and_ffn(nc, ctx, dram, x_blocks, ffn, first, banks, out_tiles)


_INS = ["L0_attn_x", "L0_attn_Wq", "L0_attn_Wk", "L0_attn_Wv", "L0_ffn_weights", "L0_ffn_scale", "L0_ffn_bias"]


def kernel(**inputs):
    import numpy as np
    import concourse.bacc as bacc
    from concourse.bass_utils import run_bass_kernel_spmd

    nc = bacc.Bacc("TRN2", target_bir_lowering=False, num_devices=1)
    arrays, args = {}, []
    for name in _INS:
        a = np.ascontiguousarray(inputs[name])
        arrays[f"in_{name}"] = a
        args.append(nc.dram_tensor(f"in_{name}", a.shape, mybir.dt.from_np(a.dtype), kind="ExternalInput").ap())
    out = nc.dram_tensor("out_x", (N, S, D), FP32, kind="ExternalOutput").ap()
    build(nc, *args, out)
    r = run_bass_kernel_spmd(nc, [arrays], core_ids=[0])
    return r.results[0]["out_x"]
```
